# Optimizing a Trainium2 kernel written in Bass

```python
import numpy as np
import jax
import jax.numpy as jnp

def _softmax(x, axis=-1):
    return jax.nn.softmax(x, axis=axis)

def _gelu(x):
    return jax.nn.gelu(x, approximate=True)

def _silu(x):
    return jax.nn.silu(x)

def _sigmoid(x):
    return jax.nn.sigmoid(x)

def _layernorm(x, axis=-1, eps=1e-05):
    m = jnp.mean(x, axis=axis, keepdims=True)
    v = jnp.var(x, axis=axis, keepdims=True)
    return (x - m) / jnp.sqrt(v + eps)

def _scatter_add(tgt, idx, src, axis=0):
    return tgt.at[idx].add(src)

def _segment_sum(src, seg, n):
    return jax.ops.segment_sum(src, seg, n)
kernel_name = 'mk_sandwich_d1_jaxref_r8_deb0f5'

def setup_inputs(seed: int=0):
    np.random.seed(seed)
    _w = jnp.asarray

    def _L0_attn_setup():
        import jax, jax.numpy as jnp
        import numpy as np
        B, S, H = (4, 512, 128)
        GAMMA = 0.96875

        def decay_mask(seq_len, gamma, dtype=jnp.float32):
            i = jnp.arange(seq_len)[:, None]
            j = jnp.arange(seq_len)[None, :]
            exp = (i - j).astype(dtype)
            return jnp.where(i >= j, jnp.power(jnp.asarray(gamma, dtype), exp), jnp.zeros((), dtype))
        key = jax.random.key(seed)
        ks = jax.random.split(key, 6)
        sc = 1.0 / np.sqrt(H)
        return {'x': jax.random.normal(ks[0], (B, S, H), dtype=jnp.float32), 'Wq': jax.random.normal(ks[1], (H, H), dtype=jnp.float32) * sc, 'bq': jax.random.normal(ks[2], (H,), dtype=jnp.float32) * 0.01, 'Wk': jax.random.normal(ks[3], (H, H), dtype=jnp.float32) * sc, 'bk': jax.random.normal(ks[4], (H,), dtype=jnp.float32) * 0.01, 'Wv': jax.random.normal(ks[5], (H, H), dtype=jnp.float32) * sc}
    _L0_attn_in = _L0_attn_setup()

    def _L0_ffn_setup():
        import jax, jax.numpy as jnp
        import numpy as np
        D_IN, D_HID = (128, 512)

        def _ternary(key, shape):
            return jax.random.randint(key, shape, -1, 2).astype(jnp.float32)

        def _tlin(x, w, s):
            return jnp.einsum('bsi,oi->bso', x, w) * s
        key = jax.random.key(seed)
        ks = jax.random.split(key, 12)
        inv = lambda fan: 1.0 / np.sqrt(fan).astype(np.float32)
        return {'x': jax.random.normal(ks[0], (4, 256, D_IN), dtype=jnp.float32), 'w1_w': _ternary(ks[1], (D_HID, D_IN)), 'w1_s': jax.random.uniform(ks[2], (D_HID,), dtype=jnp.float32) * inv(D_IN), 'w2_w': _ternary(ks[3], (D_HID, D_IN)), 'w2_s': jax.random.uniform(ks[4], (D_HID,), dtype=jnp.float32) * inv(D_IN), 'h1_w': _ternary(ks[5], (D_HID, D_HID)), 'h1_s': jax.random.uniform(ks[6], (D_HID,), dtype=jnp.float32) * inv(D_HID), 'h2_w': _ternary(ks[7], (D_HID, D_HID)), 'h2_s': jax.random.uniform(ks[8], (D_HID,), dtype=jnp.float32) * inv(D_HID), 'w3_w': _ternary(ks[9], (D_IN, D_HID)), 'w3_s': jax.random.uniform(ks[10], (D_IN,), dtype=jnp.float32) * inv(D_HID)}
    _L0_ffn_in = _L0_ffn_setup()
    _d = {'L0_attn_x': _L0_attn_in['x'], 'L0_attn_Wq': _L0_attn_in['Wq'], 'L0_attn_bq': _L0_attn_in['bq'], 'L0_attn_Wk': _L0_attn_in['Wk'], 'L0_attn_bk': _L0_attn_in['bk'], 'L0_attn_Wv': _L0_attn_in['Wv'], 'L0_ffn_w1_w': _L0_ffn_in['w1_w'], 'L0_ffn_w1_s': _L0_ffn_in['w1_s'], 'L0_ffn_w2_w': _L0_ffn_in['w2_w'], 'L0_ffn_w2_s': _L0_ffn_in['w2_s'], 'L0_ffn_h1_w': _L0_ffn_in['h1_w'], 'L0_ffn_h1_s': _L0_ffn_in['h1_s'], 'L0_ffn_h2_w': _L0_ffn_in['h2_w'], 'L0_ffn_h2_s': _L0_ffn_in['h2_s'], 'L0_ffn_w3_w': _L0_ffn_in['w3_w'], 'L0_ffn_w3_s': _L0_ffn_in['w3_s']}
    _x0 = _d['L0_attn_x']
    _d['L0_attn_x'] = jax.random.normal(jax.random.fold_in(jax.random.key(seed), 1), (8, 1024, 128), dtype=_x0.dtype)
    del _x0
    return _d

def reference(L0_attn_x, L0_attn_Wq, L0_attn_bq, L0_attn_Wk, L0_attn_bk, L0_attn_Wv, L0_ffn_w1_w, L0_ffn_w1_s, L0_ffn_w2_w, L0_ffn_w2_s, L0_ffn_h1_w, L0_ffn_h1_s, L0_ffn_h2_w, L0_ffn_h2_s, L0_ffn_w3_w, L0_ffn_w3_s):

    def _L0_attn_ref(x, Wq, bq, Wk, bk, Wv):
        import jax, jax.numpy as jnp
        import numpy as np
        B, S, H = (4, 512, 128)
        GAMMA = 0.96875

        def decay_mask(seq_len, gamma, dtype=jnp.float32):
            i = jnp.arange(seq_len)[:, None]
            j = jnp.arange(seq_len)[None, :]
            exp = (i - j).astype(dtype)
            return jnp.where(i >= j, jnp.power(jnp.asarray(gamma, dtype), exp), jnp.zeros((), dtype))
        seq_len = x.shape[1]
        q = jnp.einsum('bsh,oh->bso', x, Wq) + bq
        k = jnp.einsum('bsh,oh->bso', x, Wk) + bk
        v = jnp.einsum('bsh,oh->bso', x, Wv)
        D = decay_mask(seq_len, GAMMA, x.dtype)
        scores = jnp.einsum('bqh,bkh->bqk', q, k) * D[None]
        return jnp.einsum('bqk,bkh->bqh', scores, v)

    def _L0_ffn_ref(x, w1_w, w1_s, w2_w, w2_s, h1_w, h1_s, h2_w, h2_s, w3_w, w3_s):
        import jax, jax.numpy as jnp
        import numpy as np
        D_IN, D_HID = (128, 512)

        def _ternary(key, shape):
            return jax.random.randint(key, shape, -1, 2).astype(jnp.float32)

        def _tlin(x, w, s):
            return jnp.einsum('bsi,oi->bso', x, w) * s
        h = jax.nn.silu(_tlin(x, w1_w, w1_s)) * _tlin(x, w2_w, w2_s)
        h = jax.nn.gelu(_tlin(h, h1_w, h1_s), approximate=False)
        h = jax.nn.gelu(_tlin(h, h2_w, h2_s), approximate=False)
        return _tlin(h, w3_w, w3_s)
    x = L0_attn_x
    x = x + _layernorm(_L0_attn_ref(_layernorm(x, axis=-1), L0_attn_Wq, L0_attn_bq, L0_attn_Wk, L0_attn_bk, L0_attn_Wv), axis=-1)
    x = x + _layernorm(_L0_ffn_ref(_layernorm(x, axis=-1), L0_ffn_w1_w, L0_ffn_w1_s, L0_ffn_w2_w, L0_ffn_w2_s, L0_ffn_h1_w, L0_ffn_h1_s, L0_ffn_h2_w, L0_ffn_h2_s, L0_ffn_w3_w, L0_ffn_w3_s), axis=-1)
    return x

_drawn_inputs = setup_inputs


def setup_inputs(seed=0):
    import zlib

    import numpy as np

    out = dict(_drawn_inputs(seed))
    spreads = {}
    factors = {'L0_attn_bq': 6.818, 'L0_attn_bk': 8.0}
    for name, (base, spread) in spreads.items():
        noise = np.random.default_rng([zlib.crc32(name.encode()), seed]).standard_normal(out[name].shape)
        drawn = base * np.exp(spread * noise) if base else spread * noise
        out[name] = jnp.asarray(drawn.astype(out[name].dtype))
    for name, factor in factors.items():
        out[name] = (out[name] * factor).astype(out[name].dtype)
    return out
```

```python
from contextlib import ExitStack

import numpy as np

import concourse.bass as bass
from concourse import mybir

F32 = mybir.dt.float32
F32R = mybir.dt.float32r
I32 = mybir.dt.int32
ALU = mybir.AluOpType
ACT = mybir.ActivationFunctionType

P = 128
EPS = 1e-5
GAMMA = 0.96875
CHUNKS = 4
TOK = CHUNKS * P

C_IDENT, C_TRI, C_ROWY, C_GS, C_IGS2 = 0, P, 2 * P, 3 * P, 3 * P + 1
C_COLS = 3 * P + 2
A_Q, A_K, A_V, A_BQ, A_BK = 0, P, 2 * P, 3 * P, 3 * P + 1
A_COLS = 3 * P + 2


def decay_tables():
    j = np.arange(P, dtype=np.float64)
    gs = GAMMA ** ((P - 1 - j) / 2)
    table = np.zeros((P, C_COLS), np.float64)
    table[:, C_IDENT:C_IDENT + P] = np.eye(P)
    table[:, C_TRI:C_TRI + P] = (j[:, None] <= j[None, :]) * GAMMA ** -float(P)
    table[:, C_ROWY:C_ROWY + P] = (GAMMA ** (j + 1) / gs)[None, :]
    table[:, C_GS] = gs
    table[:, C_IGS2] = gs ** -2.0
    return table.astype(np.float32)


def sandwich(nc, x_dram, table_dram, attn_w_dram, ffn_w_dram, scales_dram, out_dram, hidden):
    K = hidden // P
    TILES = x_dram.shape[0] // TOK
    G128 = GAMMA ** float(P)

    W_1, W_2 = 0, hidden
    W_H1 = 2 * hidden
    W_H2 = W_H1 + K * hidden
    W_3 = W_H2 + K * hidden
    W_COLS = W_3 + K * P
    S_1, S_2, S_H1, S_H2, S_3 = 0, K, 2 * K, 3 * K, 4 * K
    S_COLS = 4 * K + 1
    PIECES = [(W_1, W_H1), (W_H1, W_H2), (W_H2, W_3), (W_3, W_COLS)]

    x_tiles = x_dram.rearrange("(t c p) h -> t p c h", c=CHUNKS, p=P)
    out_tiles = out_dram.rearrange("(t c p) h -> t p c h", c=CHUNKS, p=P)

    with ExitStack() as ctx:
        def sb(name, shape, dt=F32):
            return ctx.enter_context(nc.sbuf_tensor(name, shape, dt))

        def sem(name):
            return ctx.enter_context(nc.semaphore(name))

        def bank(name):
            return ctx.enter_context(nc.psum_tensor(name, [P, TOK], F32))

        def split(name, shape):
            return sb(name + "_hi", shape, F32R), sb(name + "_lo", shape, F32R)

        table = sb("table", [P, C_COLS])
        attn_w = sb("attn_w", [P, A_COLS])
        scales = sb("scales", [P, S_COLS])
        w_raw = sb("w_raw", [P, W_COLS])
        w_hi, w_lo = split("w", [P, W_COLS])
        w_abs = sb("w_abs", [P, K * hidden])
        lo_sums = sb("lo_sums", [P, len(PIECES)])
        lo_sum = sb("lo_sum", [P, 1])
        warm = sb("warm", [P, 1])
        eps_col = sb("eps_col", [P, 1])
        sink = sb("sink", [P, P])
        flag = sb("flag", [P, 1])
        ones = sb("ones", [P, 1])
        half_s1 = sb("half_s1", [P, K])
        silu_s = sb("silu_s", [P, K])
        neg_half = sb("neg_half", [P, CHUNKS])
        wq_aug = sb("wq_aug", [P, P])
        wk_aug = sb("wk_aug", [P, P])
        wv_aug = sb("wv_aug", [P, P])
        a_hi, a_lo = split("a", [P, P])
        v_hi, v_lo = split("v", [P, P])

        x_in = [sb(f"x_in{b}", [P, CHUNKS, P]) for b in range(2)]
        xs = sb("xs", [P, CHUNKS, P])
        xs_hi, xs_lo = split("xs", [P, CHUNKS, P])
        xsT_hi, xsT_lo = split("xsT", [P, TOK])
        y = sb("y", [P, TOK])
        y_hi, y_lo = split("y", [P, TOK])
        state = [sb(f"state{b}", [P, CHUNKS, P]) for b in range(2)]
        state_hi, state_lo = split("state", [P, CHUNKS, P])
        scores = sb("scores", [P, TOK])
        scores_hi, scores_lo = split("scores", [P, TOK])
        r_hi, r_lo = split("r", [P, TOK])
        attn_n = sb("attn_n", [P, CHUNKS, P])
        x1 = [sb(f"x1_{b}", [P, CHUNKS, P]) for b in range(2)]
        x1_late = sb("x1_late", [P, CHUNKS, P])
        x2 = sb("x2", [P, CHUNKS, P])
        x2T_hi, x2T_lo = split("x2T", [P, TOK])
        tanh_z = [sb(f"tanh_z{i}", [P, TOK]) for i in range(2)]
        gate = [sb(f"gate{i}", [P, TOK]) for i in range(2)]
        h_a = [sb(f"h_a{i}", [P, TOK]) for i in range(2)]
        h_g = [sb(f"h_g{i}", [P, TOK]) for i in range(2)]
        ha_hi, ha_lo = split("ha", [P, K, TOK])
        hb_hi, hb_lo = split("hb", [P, K, TOK])
        hc_hi, hc_lo = split("hc", [P, K, TOK])
        ffnT = sb("ffnT", [P, TOK])
        ffn_n = sb("ffn_n", [P, CHUNKS, P])
        result = [sb(f"result{b}", [P, CHUNKS, P]) for b in range(2)]
        stats = sb("stats", [P, 4, CHUNKS, 6])
        mean_var = sb("mean_var", [P, 4, CHUNKS, 2])
        var_eps = sb("var_eps", [P, 4, CHUNKS])
        rstd = sb("rstd", [P, 4, CHUNKS])
        neg_mr = sb("neg_mr", [P, 4, CHUNKS])

        ps_att = [bank(f"ps_att{i}") for i in range(2)]
        ps_h = [bank(f"ps_h{i}") for i in range(2)]
        ps_z = [[bank(f"ps_z{p}{i}") for i in range(2)] for p in range(2)]

        table_in, attn_in, scales_in = sem("table_in"), sem("attn_in"), sem("scales_in")
        w_in = [sem(f"w_in{i}") for i in range(len(PIECES))]
        x_loaded = [sem(f"x_loaded{b}") for b in range(2)]
        stored = [sem(f"stored{b}") for b in range(2)]
        dve_setup, act_setup, pe_setup = sem("dve_setup"), sem("act_setup"), sem("pe_setup")
        w_hi_done, w_lo_done = sem("w_hi_done"), sem("w_lo_done")
        ln_stats = [sem(f"ln{i}_stats") for i in range(4)]
        ln_rstd = [sem(f"ln{i}_rstd") for i in range(4)]
        ln_bias = {i: sem(f"ln{i}_bias") for i in (1, 3)}
        xs_done, xs_hi_done, xs_lo_done = sem("xs_done"), sem("xs_hi_done"), sem("xs_lo_done")
        xsT_done, xsT_hi_done, xsT_lo_done = sem("xsT_done"), sem("xsT_hi_done"), sem("xsT_lo_done")
        y_ps, y_done, y_hi_done, y_lo_done = sem("y_ps"), sem("y_done"), sem("y_hi_done"), sem("y_lo_done")
        outer_ps, state_done = sem("outer_ps"), sem("state_done")
        state_hi_done, state_lo_done = sem("state_hi_done"), sem("state_lo_done")
        scores_ps, scores_done = sem("scores_ps"), sem("scores_done")
        scores_hi_done, scores_lo_done = sem("scores_hi_done"), sem("scores_lo_done")
        r_ps, r_hi_done, r_lo_done = sem("r_ps"), sem("r_hi_done"), sem("r_lo_done")
        attn_ps, attn_n_done, x1_done, x1_late_done = sem("attn_ps"), sem("attn_n_done"), sem("x1_done"), sem("x1_late_done")
        x2_done, x2T_ps, x2T_hi_done, x2T_lo_done = sem("x2_done"), sem("x2T_ps"), sem("x2T_hi_done"), sem("x2T_lo_done")
        z_ps, tanh_done, gate_done, silu_done = sem("z_ps"), sem("tanh_done"), sem("gate_done"), sem("silu_done")
        ha_hi_done, ha_lo_done = sem("ha_hi_done"), sem("ha_lo_done")
        h1_ps, gelu1_done, hb_hi_done, hb_lo_done = sem("h1_ps"), sem("gelu1_done"), sem("hb_hi_done"), sem("hb_lo_done")
        h2_ps, gelu2_done, hc_hi_done, hc_lo_done = sem("h2_ps"), sem("gelu2_done"), sem("hc_hi_done"), sem("hc_lo_done")
        w3_ps, ffnT_done, ffn_ps, ffn_n_done, result_done = sem("w3_ps"), sem("ffnT_done"), sem("ffn_ps"), sem("ffn_n_done"), sem("result_done")

        pool_turns, dve_turns = sem("pool_turns"), sem("dve_turns")

        def after(tile):
            q, b = tile
            return (q, 1) if b == 0 else (q + 1, 0)

        def before(tile):
            q, b = tile
            return (q - 1, 1) if b == 0 else (q, 0)

        def count(tile, per=1, upto=None):
            q, b = tile
            return q * (2 * per) + (b * per + (per if upto is None else upto))

        def wait(eng, semaphore, value):
            if not isinstance(value, int) or value > 0:
                eng.wait_ge(semaphore, value)

        def by_itself(eng, turns):
            eng.sem_inc(turns, 1)

        def steps(run_body, fori):
            run_body((0, 0))
            run_body((0, 1))
            with fori(1, TILES // 2 - 1) as q:
                run_body((q, 0))
                run_body((q, 1))
            run_body((TILES // 2 - 1, 0), attend=False)
            run_body((TILES // 2 - 1, 1), attend=False, gated=False)

        def chunk(c):
            return slice(c * P, (c + 1) * P)

        def flat(t):
            return t[:].rearrange("p c h -> p (c h)")

        block = ctx.enter_context(nc.Block())

        @block.sync
        def _(sp):
            def load(tile, q):
                wait(sp, x1_done, count((q - 1, tile)))
                sp.dma_start(x_in[tile][:], x_tiles[q * 2 + tile]).then_inc(x_loaded[tile], 16)

            def store(b, q):
                wait(sp, result_done, count((q, b)))
                sp.dma_start(out_tiles[q * 2 + b], result[b][:]).then_inc(stored[b], 16)

            load(0, 0)
            sp.dma_start(attn_w[:], attn_w_dram).then_inc(attn_in, 16)
            load(1, 0)
            for i, (lo, hi) in enumerate(PIECES):
                sp.dma_start(w_raw[:, lo:hi], ffn_w_dram[:, lo:hi]).then_inc(w_in[i], 16)
            load(0, 1)
            load(1, 1)
            with sp.Fori(2, TILES // 2) as q:
                load(0, q)
                store(0, q - 2)
                load(1, q)
                store(1, q - 2)
            for q in (TILES // 2 - 2, TILES // 2 - 1):
                store(0, q)
                store(1, q)
            sp.wait_ge(stored[0], 16 * (TILES // 2))
            sp.wait_ge(stored[1], 16 * (TILES // 2))

        @block.gpsimd
        def _(pool):
            def inverse_root(tile, i):
                wait(pool, ln_stats[i], count(tile, 3))
                nc.gpsimd.tensor_tensor(rstd[:, i, :], var_eps[:, i, :], neg_half[:], ALU.pow).then_inc(ln_rstd[i], 1)

            def round_hi(out, in_, done):
                by_itself(pool, pool_turns)
                nc.gpsimd.tensor_scalar(out, in_, 1.0, 1.0, ALU.mult, ALU.mult).then_inc(done, 1)

            def xs_rounded(tile):
                wait(pool, xs_done, count(tile))
                wait(pool, r_ps, count(before(tile)))
                round_hi(flat(xs_hi), flat(xs), xs_hi_done)

            def y_rounded(tile):
                wait(pool, y_done, count(tile))
                wait(pool, r_ps, count(before(tile)))
                round_hi(y_hi[:], y[:], y_hi_done)

            def state_rounded(tile):
                wait(pool, state_done, count(tile, CHUNKS))
                wait(pool, r_ps, count(before(tile)))
                round_hi(flat(state_hi), flat(state[tile[1]]), state_hi_done)

            def scores_rounded(tile):
                wait(pool, scores_done, count(tile))
                wait(pool, r_ps, count(before(tile)))
                round_hi(scores_hi[:], scores[:], scores_hi_done)

            def silu_rounded(tile, m):
                wait(pool, silu_done, count(tile, K, m + 1))
                wait(pool, h1_ps, count(before(tile), K))
                round_hi(ha_hi[:, m, :], h_a[m % 2][:], ha_hi_done)

            def residual1(tile):
                b = tile[1]
                wait(pool, attn_n_done, count(tile))
                wait(pool, x1_late_done, count((tile[0] - 1, b)))
                nc.gpsimd.tensor_tensor(x1[b][:], attn_n[:], x_in[b][:], ALU.add).then_inc(x1_done, 1)

            def keep_x1(tile):
                wait(pool, result_done, count(before(tile)))
                by_itself(pool, pool_turns)
                nc.gpsimd.tensor_scalar(flat(x1_late), flat(x1[tile[1]]), 1.0, 1.0, ALU.mult, ALU.mult).then_inc(x1_late_done, 1)

            def residual2(tile):
                q, b = tile
                wait(pool, ffn_n_done, count(tile))
                wait(pool, x1_late_done, count(tile))
                if not isinstance(q, int) or q > 0:
                    wait(pool, stored[b], q * 16)
                nc.gpsimd.tensor_tensor(result[b][:], ffn_n[:], x1_late[:], ALU.add).then_inc(result_done, 1)

            def body(tile, attend=True, gated=True):
                ahead2, ahead1 = (tile[0] + 1, tile[1]), after(tile)
                finish = not (isinstance(tile[0], int) and tile == (0, 0))
                if attend:
                    inverse_root(ahead2, 0)
                if attend:
                    xs_rounded(ahead2)
                if finish:
                    inverse_root(before(tile), 3)
                    residual2(before(tile))
                keep_x1(tile)
                if attend:
                    state_rounded(ahead2)
                    y_rounded(ahead2)
                    scores_rounded(ahead2)
                if gated:
                    silu_rounded(ahead1, 0)
                    silu_rounded(ahead1, 1)
                if attend:
                    inverse_root(ahead2, 1)
                    residual1(ahead2)
                if gated:
                    silu_rounded(ahead1, 2)
                if attend:
                    inverse_root(ahead2, 2)
                if gated:
                    silu_rounded(ahead1, 3)

            pool.wait_ge(dve_setup, 1)
            for tile in ((0, 0), (0, 1)):
                inverse_root(tile, 0)
                xs_rounded(tile)
                state_rounded(tile)
                y_rounded(tile)
                scores_rounded(tile)
                inverse_root(tile, 1)
                residual1(tile)
                inverse_root(tile, 2)
            for m in range(K):
                silu_rounded((0, 0), m)
            steps(body, pool.Fori)
            last = (TILES // 2 - 1, 1)
            inverse_root(last, 3)
            residual2(last)

        @block.scalar
        def _(act):
            def xsT_rounded(tile):
                wait(act, xsT_done, count(tile))
                wait(act, scores_ps, count(before(tile)))
                nc.scalar.activation(xsT_hi[:], ps_att[0][:], ACT.Copy).then_inc(xsT_hi_done, 1)

            def r_rounded(tile):
                wait(act, r_ps, count(tile))
                wait(act, attn_ps, count(before(tile)))
                nc.scalar.activation(r_hi[:], ps_att[0][:], ACT.Copy).then_inc(r_hi_done, 1)

            def x2T_rounded(tile):
                wait(act, x2T_ps, count(tile))
                wait(act, z_ps, count(before(tile), K))
                nc.scalar.activation(x2T_hi[:], ps_att[0][:], ACT.Copy).then_inc(x2T_hi_done, 1)

            def normalise(i, source, out, done):
                for c in range(CHUNKS):
                    last = nc.scalar.activation(out[:, c, :], source[:, chunk(c)], ACT.Identity,
                                                bias=neg_mr[:, i, c:c + 1], scale=rstd[:, i, c:c + 1])
                last.then_inc(done, 1)

            def attn_normed(tile):
                wait(act, ln_bias[1], count(tile))
                wait(act, x1_done, count(before(tile)))
                normalise(1, ps_att[1], attn_n, attn_n_done)

            def ffn_scaled(tile):
                wait(act, w3_ps, count(tile))
                wait(act, ffn_ps, count(before(tile)))
                nc.scalar.activation(ffnT[:], ps_z[0][1][:], ACT.Identity, scale=scales[:, S_3:S_3 + 1]).then_inc(ffnT_done, 1)

            def ffn_normed(tile):
                wait(act, ln_bias[3], count(tile))
                wait(act, result_done, count(before(tile)))
                normalise(3, ps_z[0][0], ffn_n, ffn_n_done)

            def tanh_half(tile, m):
                wait(act, z_ps, count(tile, K, m + 1))
                wait(act, gate_done, count(tile, K, m - 1))
                nc.scalar.activation(tanh_z[m % 2][:], ps_z[m % 2][0][:], ACT.Tanh,
                                     scale=half_s1[:, m:m + 1]).then_inc(tanh_done, 1)

            def gelu(tile, m, layer):
                if layer == 1:
                    ps_ready, lo_freed = h1_ps, (hb_lo_done, tile) if m >= 2 else (hc_lo_done, before(tile))
                    readers, out, s, done, hi_done = (h2_ps, count(before(tile), K)), hb_hi, S_H1, gelu1_done, hb_hi_done
                else:
                    ps_ready, lo_freed = h2_ps, (hc_lo_done, tile) if m >= 2 else (hb_lo_done, tile)
                    readers, out, s, done, hi_done = (w3_ps, count(before(tile))), hc_hi, S_H2, gelu2_done, hc_hi_done
                s_m = scales[:, s + m:s + m + 1]
                wait(act, ps_ready, count(tile, K, m + 1))
                wait(act, lo_freed[0], count(lo_freed[1], K, (m - 2) % K + 1))
                nc.scalar.activation(h_g[m % 2][:], ps_h[m % 2][:], ACT.Gelu, scale=s_m).then_inc(done, 1)
                wait(act, *readers)
                nc.scalar.activation(out[:, m, :], ps_h[m % 2][:], ACT.Gelu, scale=s_m).then_inc(hi_done, 1)

            def body(tile, attend=True, gated=True):
                ahead2, ahead1 = (tile[0] + 1, tile[1]), after(tile)
                finish = not (isinstance(tile[0], int) and tile == (0, 0))
                if finish:
                    ffn_scaled(before(tile))
                if gated:
                    x2T_rounded(ahead1)
                gelu(tile, 0, 1)
                gelu(tile, 1, 1)
                if finish:
                    ffn_normed(before(tile))
                if attend:
                    xsT_rounded(ahead2)
                gelu(tile, 2, 1)
                gelu(tile, 3, 1)
                gelu(tile, 0, 2)
                if gated:
                    tanh_half(ahead1, 0)
                if attend:
                    r_rounded(ahead2)
                gelu(tile, 1, 2)
                if gated:
                    tanh_half(ahead1, 1)
                gelu(tile, 2, 2)
                if attend:
                    attn_normed(ahead2)
                if gated:
                    tanh_half(ahead1, 2)
                gelu(tile, 3, 2)
                if gated:
                    tanh_half(ahead1, 3)

            act.dma_start(table[:], table_dram).then_inc(table_in, 16)
            act.dma_start(scales[:], scales_dram).then_inc(scales_in, 16)
            act.wait_ge(dve_setup, 2)
            nc.scalar.activation(warm[:], ones[:], ACT.Gelu).then_inc(act_setup, 1)
            xsT_rounded((0, 0))
            r_rounded((0, 0))
            attn_normed((0, 0))
            for i, (lo, hi) in enumerate(PIECES):
                act.wait_ge(w_lo_done, i + 1)
                if i:
                    act.wait_ge(act_setup, i + 1)
                nc.scalar.activation(w_abs[:, 0:hi - lo], w_lo[:, lo:hi].bitcast(F32), ACT.Abs,
                                     accum_out=lo_sums[:, i:i + 1]).then_inc(act_setup, 1)
            act.wait_ge(scales_in, 16)
            nc.scalar.mul(half_s1[:], scales[:, S_1:S_1 + K], 0.5).then_inc(act_setup, 1)
            x2T_rounded((0, 0))
            act.wait_ge(act_setup, len(PIECES) + 2)
            xsT_rounded((0, 1))
            r_rounded((0, 1))
            attn_normed((0, 1))
            for m in range(K):
                tanh_half((0, 0), m)
            steps(body, act.Fori)
            last = (TILES // 2 - 1, 1)
            ffn_scaled(last)
            ffn_normed(last)

        @block.vector
        def _(dve):
            sub, mult, add = ALU.subtract, ALU.mult, ALU.add

            def layer_stats(tile, i, source):
                for c in range(CHUNKS):
                    last = nc.vector.bn_stats(stats[:, i, c, :], source(c))
                last.then_inc(ln_stats[i], 1)
                dve.wait_ge(ln_stats[i], count(tile, 3, 1))
                by_itself(dve, dve_turns)
                for c in range(CHUNKS):
                    last = nc.vector.bn_aggr(mean_var[:, i, c, :], stats[:, i, c, :])
                last.then_inc(ln_stats[i], 1)
                dve.wait_ge(ln_stats[i], count(tile, 3, 2))
                factor = table[:, C_IGS2:C_IGS2 + 1] if i == 0 else ones[:]
                nc.vector.tensor_scalar(var_eps[:, i, :], mean_var[:, i, :, 1], eps_col[:], factor, add, mult).then_inc(ln_stats[i], 1)

            def norm_bias(tile, i):
                wait(dve, ln_rstd[i], count(tile))
                nc.vector.scalar_tensor_tensor(neg_mr[:, i, :], mean_var[:, i, :, 0], -1.0, rstd[:, i, :], mult, mult).then_inc(ln_bias[i], 1)

            def lo_part(out, full, hi, done):
                nc.vector.tensor_tensor(out, full, hi.bitcast(F32), sub).then_inc(done, 1)

            def x_stats(tile):
                q, b = tile
                wait(dve, x_loaded[b], (q + 1) * 16)
                layer_stats(tile, 0, lambda c: x_in[b][:, c, :])

            def xs_normed(tile):
                b = tile[1]
                wait(dve, ln_rstd[0], count(tile))
                wait(dve, xs_hi_done, count(before(tile)))
                wait(dve, xs_lo_done, count(before(tile)))
                wait(dve, xsT_done, count(before(tile)))
                for c in range(CHUNKS):
                    last = nc.vector.tensor_scalar(xs[:, c, 0:P - 1], x_in[b][:, c, 0:P - 1], mean_var[:, 0, c, 0:1],
                                                   rstd[:, 0, c:c + 1], sub, mult)
                last.then_inc(xs_done, 1)

            def xs_low(tile):
                wait(dve, xs_hi_done, count(tile))
                lo_part(flat(xs_lo), flat(xs), flat(xs_hi), xs_lo_done)

            def xsT_low(tile):
                wait(dve, xsT_hi_done, count(tile))
                lo_part(xsT_lo[:], ps_att[0][:], xsT_hi[:], xsT_lo_done)

            def state_chain(tile):
                b = tile[1]
                wait(dve, outer_ps, count(tile))
                wait(dve, state_hi_done, count(before(tile)))
                wait(dve, state_lo_done, count(before(tile)))
                for c in range(CHUNKS):
                    if c < CHUNKS - 1:
                        out = state[b][:, c + 1, :]
                    else:
                        out = state[1][:, 0, :] if b == 0 else sink[:]
                    wait(dve, state_done, count(tile, CHUNKS, c))
                    nc.vector.scalar_tensor_tensor(out, state[b][:, c, :], G128, ps_att[1][:, chunk(c)], mult, add).then_inc(state_done, 1)

            def state_low(tile):
                wait(dve, state_hi_done, count(tile))
                wait(dve, r_ps, count(before(tile)))
                lo_part(flat(state_lo), flat(state[tile[1]]), flat(state_hi), state_lo_done)

            def y_scaled(tile):
                wait(dve, y_ps, count(tile))
                wait(dve, y_hi_done, count(before(tile)))
                wait(dve, y_lo_done, count(before(tile)))
                row = table[:, None, C_ROWY:C_ROWY + P].to_broadcast([P, CHUNKS, P])
                nc.vector.tensor_tensor(y[:].rearrange("p (c i) -> p c i", c=CHUNKS),
                                        ps_att[0][:].rearrange("p (c i) -> p c i", c=CHUNKS), row, mult).then_inc(y_done, 1)

            def y_low(tile):
                wait(dve, y_hi_done, count(tile))
                wait(dve, r_ps, count(before(tile)))
                lo_part(y_lo[:], y[:], y_hi[:], y_lo_done)

            def scores_masked(tile):
                wait(dve, scores_ps, count(tile))
                wait(dve, scores_hi_done, count(before(tile)))
                wait(dve, scores_lo_done, count(before(tile)))
                tri = table[:, None, C_TRI:C_TRI + P].to_broadcast([P, CHUNKS, P])
                nc.vector.tensor_tensor(scores[:].rearrange("p (c i) -> p c i", c=CHUNKS),
                                        ps_att[1][:].rearrange("p (c i) -> p c i", c=CHUNKS), tri, mult).then_inc(scores_done, 1)

            def scores_low(tile):
                wait(dve, scores_hi_done, count(tile))
                wait(dve, r_ps, count(before(tile)))
                lo_part(scores_lo[:], scores[:], scores_hi[:], scores_lo_done)

            def r_low(tile):
                wait(dve, r_hi_done, count(tile))
                lo_part(r_lo[:], ps_att[0][:], r_hi[:], r_lo_done)

            def attn_stats(tile):
                wait(dve, attn_ps, count(tile))
                layer_stats(tile, 1, lambda c: ps_att[1][:, chunk(c)])

            def x1_stats(tile):
                wait(dve, x1_done, count(tile))
                layer_stats(tile, 2, lambda c: x1[tile[1]][:, c, :])

            def x2_normed(tile):
                wait(dve, ln_rstd[2], count(tile))
                wait(dve, x2T_ps, count(before(tile)))
                for c in range(CHUNKS):
                    last = nc.vector.tensor_scalar(x2[:, c, :], x1[tile[1]][:, c, :], mean_var[:, 2, c, 0:1],
                                                   rstd[:, 2, c:c + 1], sub, mult)
                last.then_inc(x2_done, 1)

            def x2T_low(tile):
                wait(dve, x2T_hi_done, count(tile))
                lo_part(x2T_lo[:], ps_att[0][:], x2T_hi[:], x2T_lo_done)

            def silu_gate(tile, m):
                wait(dve, tanh_done, count(tile, K, m + 1))
                wait(dve, silu_done, count(tile, K, m - 1))
                nc.vector.scalar_tensor_tensor(gate[m % 2][:], tanh_z[m % 2][:], 1.0, ps_z[m % 2][0][:], add, mult).then_inc(gate_done, 1)
                wait(dve, gate_done, count(tile, K, m + 1))
                wait(dve, ha_hi_done, count(tile, K, m - 1))
                wait(dve, ha_lo_done, count(tile, K, m - 1))
                nc.vector.scalar_tensor_tensor(h_a[m % 2][:], gate[m % 2][:], silu_s[:, m:m + 1], ps_z[m % 2][1][:], mult, mult).then_inc(silu_done, 1)

            def ha_low(tile, m):
                wait(dve, ha_hi_done, count(tile, K, m + 1))
                lo_part(ha_lo[:, m, :], h_a[m % 2][:], ha_hi[:, m, :], ha_lo_done)

            def gelu_low(tile, m, layer):
                hi, lo, hi_done, lo_done = ((hb_hi, hb_lo, hb_hi_done, hb_lo_done) if layer == 1
                                            else (hc_hi, hc_lo, hc_hi_done, hc_lo_done))
                wait(dve, hi_done, count(tile, K, m + 1))
                lo_part(lo[:, m, :], h_g[m % 2][:], hi[:, m, :], lo_done)

            def ffn_stats(tile):
                wait(dve, ffn_ps, count(tile))
                layer_stats(tile, 3, lambda c: ps_z[0][0][:, chunk(c)])

            def body(tile, attend=True, gated=True):
                ahead2, ahead1 = (tile[0] + 1, tile[1]), after(tile)
                finish = not (isinstance(tile[0], int) and tile == (0, 0))
                if attend:
                    x_stats(ahead2)
                gelu_low(tile, 0, 1)
                if gated:
                    x2T_low(ahead1)
                if attend:
                    xs_normed(ahead2)
                if finish:
                    ffn_stats(before(tile))
                if attend:
                    xs_low(ahead2)
                gelu_low(tile, 1, 1)
                if finish:
                    norm_bias(before(tile), 3)
                if attend:
                    xsT_low(ahead2)
                gelu_low(tile, 2, 1)
                if attend:
                    state_chain(ahead2)
                    y_scaled(ahead2)
                    state_low(ahead2)
                gelu_low(tile, 3, 1)
                if attend:
                    y_low(ahead2)
                    scores_masked(ahead2)
                gelu_low(tile, 0, 2)
                if attend:
                    scores_low(ahead2)
                if gated:
                    silu_gate(ahead1, 0)
                gelu_low(tile, 1, 2)
                if gated:
                    ha_low(ahead1, 0)
                if attend:
                    r_low(ahead2)
                if gated:
                    silu_gate(ahead1, 1)
                if attend:
                    attn_stats(ahead2)
                if gated:
                    ha_low(ahead1, 1)
                if attend:
                    norm_bias(ahead2, 1)
                gelu_low(tile, 2, 2)
                if gated:
                    silu_gate(ahead1, 2)
                if attend:
                    x1_stats(ahead2)
                gelu_low(tile, 3, 2)
                if gated:
                    ha_low(ahead1, 2)
                    silu_gate(ahead1, 3)
                if attend:
                    x2_normed(ahead2)
                if gated:
                    ha_low(ahead1, 3)

            nc.vector.memset(neg_half[:], -0.5).then_inc(dve_setup, 1)
            nc.vector.memset(ones[:], 1.0).then_inc(dve_setup, 1)
            nc.vector.memset(eps_col[:], EPS).then_inc(dve_setup, 1)
            nc.vector.memset(state[0][:, 0, :], 0.0).then_inc(dve_setup, 1)
            dve.wait_ge(attn_in, 16)
            for w, col, bias in ((wq_aug, A_Q, A_BQ), (wk_aug, A_K, A_BK)):
                nc.vector.tensor_copy(w[:, P - 1:P], attn_w[:, bias:bias + 1]).then_inc(dve_setup, 1)
                nc.vector.tensor_scalar(w[:, 0:P - 1], attn_w[:, col:col + P - 1], attn_w[:, col + P - 1:col + P],
                                        None, sub).then_inc(dve_setup, 1)
            nc.vector.tensor_scalar(wv_aug[:], attn_w[:, A_V:A_V + P], attn_w[:, A_V + P - 1:A_V + P],
                                    None, sub).then_inc(dve_setup, 1)
            dve.wait_ge(table_in, 16)
            for c in range(CHUNKS):
                nc.vector.tensor_copy(xs[:, c, P - 1:P], table[:, C_GS:C_GS + 1]).then_inc(dve_setup, 1)
            dve.wait_ge(dve_setup, 9 + CHUNKS)
            x_stats((0, 0))
            dve.wait_ge(pe_setup, 1)
            nc.vector.tensor_copy(a_hi[:], ps_h[0][:, 0:P]).then_inc(dve_setup, 1)
            dve.wait_ge(dve_setup, 10 + CHUNKS)
            nc.vector.tensor_tensor(a_lo[:], ps_h[0][:, 0:P], a_hi[:].bitcast(F32), sub).then_inc(dve_setup, 1)
            dve.wait_ge(pe_setup, 2)
            nc.vector.tensor_copy(v_hi[:], ps_h[1][:, 0:P]).then_inc(dve_setup, 1)
            dve.wait_ge(dve_setup, 12 + CHUNKS)
            nc.vector.tensor_tensor(v_lo[:], ps_h[1][:, 0:P], v_hi[:].bitcast(F32), sub).then_inc(dve_setup, 1)

            def attention(tile):
                xs_normed(tile)
                xs_low(tile)
                xsT_low(tile)
                state_chain(tile)
                y_scaled(tile)
                state_low(tile)
                y_low(tile)
                scores_masked(tile)
                scores_low(tile)
                r_low(tile)
                attn_stats(tile)
                norm_bias(tile, 1)
                x1_stats(tile)
                x2_normed(tile)

            def split_weights(i):
                lo, hi = PIECES[i]
                dve.wait_ge(w_in[i], 16)
                nc.vector.tensor_copy(w_hi[:, lo:hi], w_raw[:, lo:hi]).then_inc(w_hi_done, 1)
                dve.wait_ge(w_hi_done, i + 1)
                nc.vector.tensor_tensor(w_lo[:, lo:hi], w_raw[:, lo:hi], w_hi[:, lo:hi].bitcast(F32), sub).then_inc(w_lo_done, 1)

            attention((0, 0))
            for i in range(len(PIECES)):
                split_weights(i)
            x2T_low((0, 0))
            dve.wait_ge(act_setup, len(PIECES) + 1)
            nc.vector.reduce_sum(lo_sum[:], lo_sums[:], axis=mybir.AxisListType.X).then_inc(dve_setup, 1)
            dve.wait_ge(act_setup, len(PIECES) + 2)
            nc.vector.tensor_tensor(silu_s[:], half_s1[:], scales[:, S_2:S_2 + K], mult).then_inc(dve_setup, 1)
            dve.wait_ge(pe_setup, 3)
            nc.vector.tensor_copy(flag[0:1, :], ps_h[0][0:1, 0:1]).then_inc(dve_setup, 1)
            dve.wait_ge(dve_setup, 15 + CHUNKS)
            x_stats((0, 1))
            attention((0, 1))
            for m in range(K):
                silu_gate((0, 0), m)
                ha_low((0, 0), m)
            steps(body, dve.Fori)
            last = (TILES // 2 - 1, 1)
            ffn_stats(last)
            norm_bias(last, 3)

        @block.tensor
        def _(pe):
            def product(out, left, right, start, stop, exact=False):
                terms = [(0, 0), (0, 1)] if exact else [(0, 0), (0, 1), (1, 0)]
                for n, (i, j) in enumerate(terms):
                    last = nc.tensor.matmul(out, left[i], right[j], start=start and n == 0,
                                            stop=stop and n == len(terms) - 1)
                return last

            def cut(pair, *index):
                return [t[index] for t in pair]

            every = slice(None)

            def transpose4(out, source):
                for c in range(CHUNKS):
                    last = nc.tensor.transpose(out[:, chunk(c)], source(c), table[:, C_IDENT:C_IDENT + P])
                return last

            def xs_transposed(tile):
                wait(pe, xs_done, count(tile))
                wait(pe, x2T_lo_done, count(before(tile)))
                transpose4(ps_att[0], lambda c: xs[:, c, :]).then_inc(xsT_done, 1)

            def outer_products(tile):
                wait(pe, xs_lo_done, count(tile))
                wait(pe, attn_n_done, count(before(tile)))
                for c in range(CHUNKS):
                    x_c = cut((xs_hi, xs_lo), every, c, every)
                    last = product(ps_att[1][:, chunk(c)], x_c, x_c, True, True)
                last.then_inc(outer_ps, 1)

            def queries(tile):
                wait(pe, xsT_lo_done, count(tile))
                product(ps_att[0][:], [a_hi[:], a_lo[:]], [xsT_hi[:], xsT_lo[:]], True, True).then_inc(y_ps, 1)

            def score_blocks(tile):
                wait(pe, y_lo_done, count(tile))
                wait(pe, state_done, count(tile, CHUNKS))
                for c in range(CHUNKS):
                    last = product(ps_att[1][:, chunk(c)], cut((xsT_hi, xsT_lo), every, chunk(c)),
                                   cut((y_hi, y_lo), every, chunk(c)), True, True)
                last.then_inc(scores_ps, 1)

            def retained(tile):
                wait(pe, scores_lo_done, count(tile))
                wait(pe, state_lo_done, count(tile))
                for c in range(CHUNKS):
                    out = ps_att[0][:, chunk(c)]
                    first = tile[1] == 0 and c == 0
                    last = product(out, cut((xs_hi, xs_lo), every, c, every),
                                   cut((scores_hi, scores_lo), every, chunk(c)), True, first)
                    if not first:
                        last = product(out, cut((state_hi, state_lo), every, c, every),
                                       cut((y_hi, y_lo), every, chunk(c)), False, True)
                last.then_inc(r_ps, 1)

            def values(tile):
                wait(pe, r_lo_done, count(tile))
                for c in range(CHUNKS):
                    last = product(ps_att[1][:, chunk(c)], cut((r_hi, r_lo), every, chunk(c)), [v_hi[:], v_lo[:]], True, True)
                last.then_inc(attn_ps, 1)

            def x2_transposed(tile):
                wait(pe, x2_done, count(tile))
                transpose4(ps_att[0], lambda c: x2[:, c, :]).then_inc(x2T_ps, 1)

            def weight(column, m, k=0):
                at = column + k * hidden + m * P
                return [w_hi[:, at:at + P], w_lo[:, at:at + P]]

            def ffn_parts(exact):
                def gated_layer(tile, m):
                    if m == 0:
                        wait(pe, x2T_lo_done, count(tile))
                        wait(pe, ffn_n_done, count((tile[0] - 1, tile[1])))
                    wait(pe, silu_done, count(tile, K, m - 1))
                    for i, column in enumerate((W_1, W_2)):
                        last = product(ps_z[m % 2][i][:], weight(column, m), [x2T_hi[:], x2T_lo[:]], True, True, exact)
                    last.then_inc(z_ps, 1)

                def hidden_layer(tile, m, layer):
                    if layer == 1:
                        parts, ready, column, done = (ha_hi, ha_lo), ha_lo_done, W_H1, h1_ps
                        freed = (hb_hi_done, tile) if m >= 2 else (hc_hi_done, before(tile))
                    else:
                        parts, ready, column, done = (hb_hi, hb_lo), hb_lo_done, W_H2, h2_ps
                        freed = (hc_hi_done, tile) if m >= 2 else (hb_hi_done, tile)
                    wait(pe, freed[0], count(freed[1], K, (m - 2) % K + 1))
                    for k in range(K):
                        if m == 0:
                            wait(pe, ready, count(tile, K, k + 1))
                        last = product(ps_h[m % 2][:], weight(column, m, k), cut(parts, every, k, every), k == 0, k == K - 1, exact)
                    last.then_inc(done, 1)

                def last_layer(tile, gated):
                    if gated:
                        wait(pe, silu_done, count(after(tile), K, 3))
                    for k in range(K):
                        wait(pe, hc_lo_done, count(tile, K, k + 1))
                        at = W_3 + k * P
                        last = product(ps_z[0][1][:], [w_hi[:, at:at + P], w_lo[:, at:at + P]],
                                       cut((hc_hi, hc_lo), every, k, every), k == 0, k == K - 1, exact)
                    last.then_inc(w3_ps, 1)

                def ffn_transposed(tile):
                    wait(pe, ffnT_done, count(tile))
                    transpose4(ps_z[0][0], lambda c: ffnT[:, chunk(c)]).then_inc(ffn_ps, 1)

                def body(tile, attend=True, gated=True):
                    ahead2, ahead1 = (tile[0] + 1, tile[1]), after(tile)
                    finish = not (isinstance(tile[0], int) and tile == (0, 0))
                    hidden_layer(tile, 0, 1)
                    if finish:
                        ffn_transposed(before(tile))
                    hidden_layer(tile, 1, 1)
                    if attend:
                        xs_transposed(ahead2)
                    hidden_layer(tile, 2, 1)
                    if attend:
                        outer_products(ahead2)
                        queries(ahead2)
                    hidden_layer(tile, 3, 1)
                    if attend:
                        score_blocks(ahead2)
                    hidden_layer(tile, 0, 2)
                    if gated:
                        gated_layer(ahead1, 0)
                    if attend:
                        retained(ahead2)
                    hidden_layer(tile, 1, 2)
                    if gated:
                        gated_layer(ahead1, 1)
                    if attend:
                        values(ahead2)
                    hidden_layer(tile, 2, 2)
                    if gated:
                        gated_layer(ahead1, 2)
                    hidden_layer(tile, 3, 2)
                    if gated:
                        gated_layer(ahead1, 3)
                    last_layer(tile, gated)
                    if attend:
                        x2_transposed(ahead2)

                for m in range(K):
                    gated_layer((0, 0), m)
                steps(body, pe.Fori)
                ffn_transposed((TILES // 2 - 1, 1))

            pe.wait_ge(dve_setup, 9)
            pe.wait_ge(table_in, 16)
            nc.tensor.matmul(ps_h[0][:, 0:P], wq_aug[:], wk_aug[:], start=True, stop=True).then_inc(pe_setup, 1)
            nc.tensor.transpose(ps_h[1][:, 0:P], wv_aug[:], table[:, C_IDENT:C_IDENT + P]).then_inc(pe_setup, 1)
            xs_transposed((0, 0))
            outer_products((0, 0))
            pe.wait_ge(dve_setup, 13 + CHUNKS)
            queries((0, 0))
            score_blocks((0, 0))
            retained((0, 0))
            values((0, 0))
            x2_transposed((0, 0))
            pe.wait_ge(dve_setup, 14 + CHUNKS)
            nc.tensor.matmul(ps_h[0][0:1, 0:1], lo_sum[:], ones[:], start=True, stop=True).then_inc(pe_setup, 1)
            xs_transposed((0, 1))
            outer_products((0, 1))
            queries((0, 1))
            score_blocks((0, 1))
            retained((0, 1))
            values((0, 1))
            x2_transposed((0, 1))
            pe.wait_ge(dve_setup, 16 + CHUNKS)
            any_lo = pe.value_load(flag[0:1, 0:1].bitcast(I32))
            with pe.If(any_lo != 0):
                ffn_parts(exact=False)
            with pe.Else():
                ffn_parts(exact=True)


def kernel(**inputs):
    import concourse.bacc as _bacc
    from concourse.bass_utils import run_bass_kernel_spmd as _run

    a = {name.removeprefix("L0_"): np.asarray(value) for name, value in inputs.items()}
    batch, seq, d = a["attn_x"].shape
    hidden = a["ffn_w1_w"].shape[0]
    k = hidden // P

    def by_input(w):
        return w.T.reshape(-1, P, w.shape[0]).transpose(1, 0, 2).reshape(P, -1)

    def by_partition(s):
        return s.reshape(-1, P).T

    arrays = {
        "x": a["attn_x"].reshape(batch * seq, d),
        "table": decay_tables(),
        "attn_w": np.concatenate([a["attn_Wq"], a["attn_Wk"], a["attn_Wv"], a["attn_bq"][:, None], a["attn_bk"][:, None]], axis=1),
        "ffn_w": np.concatenate([by_input(a[f"ffn_{n}_w"]) for n in ("w1", "w2", "h1", "h2", "w3")], axis=1),
        "scales": np.concatenate([by_partition(a[f"ffn_{n}_s"]) for n in ("w1", "w2", "h1", "h2", "w3")], axis=1),
    }
    arrays = {f"in_{n}": np.ascontiguousarray(v) for n, v in arrays.items()}
    nc = _bacc.Bacc("TRN2", target_bir_lowering=False, num_devices=1)
    args = [nc.dram_tensor(n, v.shape, F32, kind="ExternalInput").ap() for n, v in arrays.items()]
    out = nc.dram_tensor("out_0", (batch * seq, d), F32, kind="ExternalOutput").ap()
    sandwich(nc, *args, out, hidden)
    r = _run(nc, [arrays], core_ids=[0])
    return r.results[0]["out_0"].reshape(batch, seq, d)
```

```python
from contextlib import ExitStack

import numpy as np

import concourse.bass as bass
from concourse import mybir

F32 = mybir.dt.float32
F32R = mybir.dt.float32r
I32 = mybir.dt.int32
ALU = mybir.AluOpType
ACT = mybir.ActivationFunctionType

P = 128
EPS = 1e-5
GAMMA = 0.96875
CHUNKS = 4
TOK = CHUNKS * P

C_IDENT, C_TRI, C_GS, C_IGS2, C_EPS2 = 0, P, 2 * P, 2 * P + 1, 2 * P + 2
C_COLS = 2 * P + 3
A_Q, A_K, A_V, A_BQ, A_BK = 0, P, 2 * P, 3 * P, 3 * P + 1
A_COLS = 3 * P + 2


def decay_tables():
    j = np.arange(P, dtype=np.float64)
    gs = GAMMA ** ((P - 1 - j) / 2)
    table = np.zeros((P, C_COLS), np.float64)
    table[:, C_IDENT:C_IDENT + P] = np.eye(P)
    table[:, C_TRI:C_TRI + P] = (j[:, None] <= j[None, :]) * GAMMA ** -float(P)
    table[:, C_GS] = gs
    table[:, C_IGS2] = gs ** -2.0
    table[:, C_EPS2] = EPS * (gs / GAMMA ** (j + 1)) ** 2
    return table.astype(np.float32)


def sandwich(nc, x_dram, table_dram, attn_w_dram, ffn_w_dram, scales_dram, out_dram, hidden):
    K = hidden // P
    TILES = x_dram.shape[0] // TOK
    G128 = GAMMA ** float(P)

    W_1, W_2 = 0, hidden
    W_H1 = 2 * hidden
    W_H2 = W_H1 + K * hidden
    W_3 = W_H2 + K * hidden
    W_COLS = W_3 + K * P
    S_1, S_2, S_H1, S_H2, S_3 = 0, K, 2 * K, 3 * K, 4 * K
    S_COLS = 4 * K + 1
    PIECES = [(W_1, W_H1), (W_H1, W_H2), (W_H2, W_3), (W_3, W_COLS)]

    x_tiles = x_dram.rearrange("(t c p) h -> t p c h", c=CHUNKS, p=P)
    out_tiles = out_dram.rearrange("(t c p) h -> t p c h", c=CHUNKS, p=P)

    with ExitStack() as ctx:
        def sb(name, shape, dt=F32):
            return ctx.enter_context(nc.sbuf_tensor(name, shape, dt))

        def sem(name):
            return ctx.enter_context(nc.semaphore(name))

        def bank(name):
            return ctx.enter_context(nc.psum_tensor(name, [P, TOK], F32))

        def split(name, shape):
            return sb(name + "_hi", shape, F32R), sb(name + "_lo", shape, F32R)

        table = sb("table", [P, C_COLS])
        attn_w = sb("attn_w", [P, A_COLS])
        scales = sb("scales", [P, S_COLS])
        w_raw = sb("w_raw", [P, W_COLS])
        w_hi, w_lo = split("w", [P, W_COLS])
        w_abs = sb("w_abs", [P, K * hidden])
        lo_sums = sb("lo_sums", [P, len(PIECES)])
        lo_sum = sb("lo_sum", [P, 1])
        warm = sb("warm", [P, 1])
        eps_col = sb("eps_col", [P, 1])
        flag = sb("flag", [P, 1])
        ones = sb("ones", [P, 1])
        half_s1 = sb("half_s1", [P, K])
        silu_s = sb("silu_s", [P, K])
        neg_half = sb("neg_half", [P, CHUNKS])
        wq_aug = sb("wq_aug", [P, P])
        wk_aug = sb("wk_aug", [P, P])
        wv_aug = sb("wv_aug", [P, P])
        a_hi, a_lo = split("a", [P, P])
        v_hi, v_lo = split("v", [P, P])

        x_in = [sb(f"x_in{b}", [P, CHUNKS, P]) for b in range(2)]
        xs = sb("xs", [P, CHUNKS, P])
        xs_hi, xs_lo = split("xs", [P, CHUNKS, P])
        xsT_hi, xsT_lo = split("xsT", [P, TOK])
        y_hi, y_lo = split("y", [P, TOK])
        state = [sb(f"state{b}", [P, CHUNKS, P]) for b in range(2)]
        state_hi, state_lo = split("state", [P, CHUNKS, P])
        scores = sb("scores", [P, TOK])
        scores_hi, scores_lo = split("scores", [P, TOK])
        r_hi, r_lo = split("r", [P, TOK])
        attn_n = sb("attn_n", [P, CHUNKS, P])
        x1 = [sb(f"x1_{b}", [P, CHUNKS, P]) for b in range(2)]
        x1_late = sb("x1_late", [P, CHUNKS, P])
        x2 = sb("x2", [P, CHUNKS, P])
        x2T_hi, x2T_lo = split("x2T", [P, TOK])
        tanh_z = [sb(f"tanh_z{i}", [P, TOK]) for i in range(2)]
        gate = [sb(f"gate{i}", [P, TOK]) for i in range(2)]
        h_a = [sb(f"h_a{i}", [P, TOK]) for i in range(2)]
        h_g = [sb(f"h_g{m}", [P, TOK]) for m in range(K)]
        ha_hi, ha_lo = split("ha", [P, K, TOK])
        hb_hi, hb_lo = split("hb", [P, K, TOK])
        hc_hi, hc_lo = split("hc", [P, K, TOK])
        ffnT = sb("ffnT", [P, TOK])
        ffn_n = sb("ffn_n", [P, CHUNKS, P])
        result = [sb(f"result{b}", [P, CHUNKS, P]) for b in range(2)]
        stats = sb("stats", [P, 4, CHUNKS, 6])
        mean_var = sb("mean_var", [P, 4, CHUNKS, 2])
        var_eps = sb("var_eps", [P, 4, CHUNKS])
        rstd = sb("rstd", [P, 4, CHUNKS])
        neg_mr = sb("neg_mr", [P, 4, CHUNKS])

        ps_att = [bank(f"ps_att{i}") for i in range(2)]
        ps_h = [bank(f"ps_h{i}") for i in range(2)]
        ps_z = [[bank(f"ps_z{p}{i}") for i in range(2)] for p in range(2)]

        table_in, attn_in, scales_in = sem("table_in"), sem("attn_in"), sem("scales_in")
        w_in = [sem(f"w_in{i}") for i in range(len(PIECES))]
        x_loaded = [sem(f"x_loaded{b}") for b in range(2)]
        stored = [sem(f"stored{b}") for b in range(2)]
        consts_done, aug_done, gs_done = sem("consts_done"), sem("aug_done"), sem("gs_done")
        av_ps, av_done = sem("av_ps"), sem("av_done")
        half_s1_done, silu_s_done = sem("half_s1_done"), sem("silu_s_done")
        lo_sums_done, lo_sum_done, flag_ps, flag_done = sem("lo_sums_done"), sem("lo_sum_done"), sem("flag_ps"), sem("flag_done")
        w_hi_done = sem("w_hi_done")
        w_lo_done = [sem(f"w_lo_done{i}") for i in range(len(PIECES))]
        ln_stats = [sem(f"ln{i}_stats") for i in range(4)]
        ln_rstd = [sem(f"ln{i}_rstd") for i in range(4)]
        ln_bias = {i: sem(f"ln{i}_bias") for i in (1, 3)}
        xs_done, xs_hi_done, xs_lo_done = sem("xs_done"), sem("xs_hi_done"), sem("xs_lo_done")
        xsT_done, xsT_hi_done, xsT_lo_done = sem("xsT_done"), sem("xsT_hi_done"), sem("xsT_lo_done")
        y_ps, y_hi_done, y_lo_done = sem("y_ps"), sem("y_hi_done"), sem("y_lo_done")
        outer_ps, state_done = sem("outer_ps"), sem("state_done")
        state_hi_done, state_lo_done = sem("state_hi_done"), sem("state_lo_done")
        scores_ps, scores_done = sem("scores_ps"), sem("scores_done")
        scores_hi_done, scores_lo_done = sem("scores_hi_done"), sem("scores_lo_done")
        r_ps, r_hi_done, r_lo_done = sem("r_ps"), sem("r_hi_done"), sem("r_lo_done")
        attn_ps, attn_n_done, x1_done, x1_late_done = sem("attn_ps"), sem("attn_n_done"), sem("x1_done"), sem("x1_late_done")
        x2_done, x2T_ps, x2T_hi_done, x2T_lo_done = sem("x2_done"), sem("x2T_ps"), sem("x2T_hi_done"), sem("x2T_lo_done")
        z_ps, tanh_done, gate_done, silu_done = sem("z_ps"), sem("tanh_done"), sem("gate_done"), sem("silu_done")
        ha_hi_done, ha_lo_done = sem("ha_hi_done"), sem("ha_lo_done")
        h1_ps, gelu1_done, hb_hi_done, hb_lo_done = sem("h1_ps"), sem("gelu1_done"), sem("hb_hi_done"), sem("hb_lo_done")
        h2_ps, gelu2_done, hc_hi_done, hc_lo_done = sem("h2_ps"), sem("gelu2_done"), sem("hc_hi_done"), sem("hc_lo_done")
        hb_lo_last, hc_lo_last = sem("hb_lo_last"), sem("hc_lo_last")
        w3_ps, ffnT_done, ffn_ps, ffn_n_done, result_done = sem("w3_ps"), sem("ffnT_done"), sem("ffn_ps"), sem("ffn_n_done"), sem("result_done")

        last_n_done, last_result_done = sem("last_n_done"), sem("last_result_done")

        pool_turns, dve_turns = sem("pool_turns"), sem("dve_turns")

        def after(tile):
            q, b = tile
            return (q, 1) if b == 0 else (q + 1, 0)

        def before(tile):
            q, b = tile
            return (q - 1, 1) if b == 0 else (q, 0)

        def count(tile, per=1, upto=None):
            q, b = tile
            return q * (2 * per) + (b * per + (per if upto is None else upto))

        LAST = (TILES // 2 - 1, 1)

        STEADY_BANKS = dict(x=ps_att[0], y=ps_att[0], outer=ps_att[1], scores=ps_att[1], r=ps_att[0], attn=ps_att[1])
        FIRST_BANKS = [dict(x=ps_att[0], y=ps_h[1], outer=ps_z[0][0], scores=ps_z[1][0], r=ps_att[0], attn=ps_att[1]),
                       dict(x=ps_h[0], y=ps_h[1], outer=ps_z[0][1], scores=ps_z[1][1], r=ps_h[0], attn=ps_att[1])]

        def count_chain(tile, upto=None):
            q, b = tile
            return q * (2 * CHUNKS - 1) + (b * CHUNKS + (CHUNKS - b if upto is None else upto))

        def is_number(tile, number):
            return isinstance(tile[0], int) and tile[0] * 2 + tile[1] == number

        def first_sequence(tile):
            return isinstance(tile[0], int) and tile[0] == 0

        def att_bank(tile, stage):
            return (FIRST_BANKS[tile[1]] if first_sequence(tile) else STEADY_BANKS)[stage]

        def low_done(layer, tile, m):
            by_pool, by_dve = (hb_lo_done, hb_lo_last) if layer == 1 else (hc_lo_done, hc_lo_last)
            return (by_dve, count(tile)) if m == K - 1 else (by_pool, count(tile, K - 1, m + 1))

        def wait(eng, semaphore, value):
            if not isinstance(value, int) or value > 0:
                eng.wait_ge(semaphore, value)

        def by_itself(eng, turns):
            eng.sem_inc(turns, 1)

        def steps(run_body, fori):
            run_body((0, 0))
            run_body((0, 1))
            with fori(1, TILES // 2 - 1) as q:
                run_body((q, 0))
                run_body((q, 1))
            run_body((TILES // 2 - 1, 0), attend=False)
            run_body((TILES // 2 - 1, 1), attend=False, gated=False)

        def chunk(c):
            return slice(c * P, (c + 1) * P)

        def flat(t):
            return t[:].rearrange("p c h -> p (c h)")

        def low_parts(i):
            return (PIECES[i][1] - PIECES[i][0]) // TOK

        def split_low(eng, ops, i, parts=None):
            eng.wait_ge(w_hi_done, i + 1)
            for part in range(low_parts(i)) if parts is None else parts:
                at = PIECES[i][0] + part * TOK
                ops.tensor_tensor(w_lo[:, at:at + TOK], w_raw[:, at:at + TOK], w_hi[:, at:at + TOK].bitcast(F32), ALU.subtract).then_inc(w_lo_done[i], 1)

        block = ctx.enter_context(nc.Block())

        @block.sync
        def _(sp):
            def load(tile, q):
                wait(sp, x1_done, count((q - 1, tile)))
                sp.dma_start(x_in[tile][:], x_tiles[q * 2 + tile]).then_inc(x_loaded[tile], 16)

            def store(b, q):
                wait(sp, result_done, count((q, b)))
                sp.dma_start(out_tiles[q * 2 + b], result[b][:]).then_inc(stored[b], 16)

            load(0, 0)
            sp.dma_start(attn_w[:], attn_w_dram).then_inc(attn_in, 16)
            load(1, 0)
            for i, (lo, hi) in enumerate(PIECES):
                sp.dma_start(w_raw[:, lo:hi], ffn_w_dram[:, lo:hi]).then_inc(w_in[i], 16)
            load(0, 1)
            load(1, 1)
            with sp.Fori(2, TILES // 2) as q:
                load(0, q)
                store(0, q - 2)
                load(1, q)
                store(1, q - 2)
            store(0, TILES // 2 - 2)
            store(1, TILES // 2 - 2)
            store(0, TILES // 2 - 1)
            for h in range(2):
                part = slice(2 * h, 2 * h + 2)
                sp.wait_ge(last_result_done, h + 1)
                sp.dma_start(out_tiles[TILES - 1][:, part, :], result[1][:, part, :]).then_inc(stored[1], 16)
            sp.wait_ge(stored[0], 16 * (TILES // 2))
            sp.wait_ge(stored[1], 16 * (TILES // 2 + 1))

        @block.gpsimd
        def _(pool):
            def inverse_root(tile, i):
                wait(pool, ln_stats[i], count(tile, 3))
                nc.gpsimd.tensor_tensor(rstd[:, i, :], var_eps[:, i, :], neg_half[:], ALU.pow).then_inc(ln_rstd[i], 1)

            def round_hi(out, in_, done):
                by_itself(pool, pool_turns)
                nc.gpsimd.tensor_scalar(out, in_, 1.0, 1.0, ALU.mult, ALU.mult).then_inc(done, 1)

            def xs_rounded(tile):
                wait(pool, xs_done, count(tile))
                wait(pool, r_ps, count(before(tile)))
                round_hi(flat(xs_hi), flat(xs), xs_hi_done)

            def state_rounded(tile):
                wait(pool, state_done, count_chain(tile))
                wait(pool, r_ps, count(before(tile)))
                round_hi(flat(state_hi), flat(state[tile[1]]), state_hi_done)

            def scores_rounded(tile):
                wait(pool, scores_done, count(tile))
                wait(pool, r_ps, count(before(tile)))
                round_hi(scores_hi[:], scores[:], scores_hi_done)

            def silu_rounded(tile, m):
                wait(pool, silu_done, count(tile, K, m + 1))
                wait(pool, h1_ps, count(before(tile), K))
                round_hi(ha_hi[:, m, :], h_a[m % 2][:], ha_hi_done)

            def gelu_low(tile, m, layer):
                hi, lo, hi_done, lo_done = ((hb_hi, hb_lo, hb_hi_done, hb_lo_done) if layer == 1
                                            else (hc_hi, hc_lo, hc_hi_done, hc_lo_done))
                wait(pool, hi_done, count(tile, K, m + 1))
                nc.gpsimd.tensor_tensor(lo[:, m, :], h_g[m][:], hi[:, m, :].bitcast(F32), ALU.subtract).then_inc(lo_done, 1)

            def residual1(tile):
                b = tile[1]
                wait(pool, attn_n_done, count(tile))
                wait(pool, x1_late_done, count((tile[0] - 1, b)))
                nc.gpsimd.tensor_tensor(x1[b][:], attn_n[:], x_in[b][:], ALU.add).then_inc(x1_done, 1)

            def keep_x1(tile):
                wait(pool, result_done, count(before(tile)))
                by_itself(pool, pool_turns)
                nc.gpsimd.tensor_scalar(flat(x1_late), flat(x1[tile[1]]), 1.0, 1.0, ALU.mult, ALU.mult).then_inc(x1_late_done, 1)

            def residual2(tile):
                q, b = tile
                wait(pool, ffn_n_done, count(tile))
                wait(pool, x1_late_done, count(tile))
                if not isinstance(q, int) or q > 0:
                    wait(pool, stored[b], q * 16)
                nc.gpsimd.tensor_tensor(result[b][:], ffn_n[:], x1_late[:], ALU.add).then_inc(result_done, 1)

            def body(tile, attend=True, gated=True):
                ahead2, ahead1 = (tile[0] + 1, tile[1]), after(tile)
                finish = not is_number(tile, 0)
                if attend:
                    inverse_root(ahead2, 0)
                if gated:
                    inverse_root(ahead1, 1)
                gelu_low(tile, 0, 1)
                if attend:
                    xs_rounded(ahead2)
                if gated:
                    residual1(ahead1)
                gelu_low(tile, 1, 1)
                if not gated:
                    inverse_root(before(tile), 3)
                gelu_low(tile, 2, 1)
                if gated:
                    inverse_root(ahead1, 2)
                    if finish:
                        inverse_root(before(tile), 3)
                gelu_low(tile, 0, 2)
                if attend:
                    state_rounded(ahead2)
                if attend:
                    scores_rounded(ahead2)
                gelu_low(tile, 1, 2)
                if gated:
                    silu_rounded(ahead1, 0)
                    silu_rounded(ahead1, 1)
                if attend:
                    if finish:
                        residual2(before(tile))
                    keep_x1(tile)
                    gelu_low(tile, 2, 2)
                    silu_rounded(ahead1, 2)
                    silu_rounded(ahead1, 3)
                elif gated:
                    residual2(before(tile))
                    silu_rounded(ahead1, 2)
                    silu_rounded(ahead1, 3)
                    gelu_low(tile, 2, 2)
                    keep_x1(tile)
                else:
                    gelu_low(tile, 2, 2)
                    residual2(before(tile))
                    keep_x1(tile)

            pool.wait_ge(consts_done, 1)
            t0, t1 = (0, 0), (0, 1)
            inverse_root(t0, 0)
            xs_rounded(t0)
            state_rounded(t0)
            scores_rounded(t0)
            inverse_root(t1, 0)
            split_low(pool, nc.gpsimd, 0)
            split_low(pool, nc.gpsimd, 1, (0,))
            xs_rounded(t1)
            split_low(pool, nc.gpsimd, 1, (1, 2, 3))
            inverse_root(t0, 1)
            state_rounded(t1)
            residual1(t0)
            scores_rounded(t1)
            inverse_root(t0, 2)
            for m in range(K):
                silu_rounded(t0, m)
            steps(body, pool.Fori)
            inverse_root(LAST, 3)

        @block.scalar
        def _(act):
            def xsT_rounded(tile):
                wait(act, xsT_done, count(tile))
                wait(act, scores_ps, count(before(tile)))
                nc.scalar.activation(xsT_hi[:], att_bank(tile, "x")[:], ACT.Copy).then_inc(xsT_hi_done, 1)

            def y_rounded(tile):
                wait(act, y_ps, count(tile))
                wait(act, r_ps, count(before(tile)))
                nc.scalar.activation(y_hi[:], att_bank(tile, "y")[:], ACT.Copy).then_inc(y_hi_done, 1)

            def r_rounded(tile):
                wait(act, r_ps, count(tile))
                wait(act, attn_ps, count(before(tile)))
                nc.scalar.activation(r_hi[:], att_bank(tile, "r")[:], ACT.Copy).then_inc(r_hi_done, 1)

            def x2T_rounded(tile):
                wait(act, x2T_ps, count(tile))
                wait(act, z_ps, count(before(tile), K))
                nc.scalar.activation(x2T_hi[:], ps_att[0][:], ACT.Copy).then_inc(x2T_hi_done, 1)

            def normalise(i, source, out, done):
                for c in range(CHUNKS):
                    last = nc.scalar.activation(out[:, c, :], source[:, chunk(c)], ACT.Identity,
                                                bias=neg_mr[:, i, c:c + 1], scale=rstd[:, i, c:c + 1])
                last.then_inc(done, 1)

            def attn_normed(tile):
                wait(act, ln_bias[1], count(tile))
                wait(act, x1_done, count(before(tile)))
                normalise(1, att_bank(tile, "attn"), attn_n, attn_n_done)

            def ffn_scaled(tile):
                wait(act, w3_ps, count(tile))
                wait(act, ffn_ps, count(before(tile)))
                nc.scalar.activation(ffnT[:], ps_z[0][1][:], ACT.Identity, scale=scales[:, S_3:S_3 + 1]).then_inc(ffnT_done, 1)

            def ffn_normed(tile):
                wait(act, ln_bias[3], count(tile))
                wait(act, result_done, count(before(tile)))
                normalise(3, ps_z[0][0], ffn_n, ffn_n_done)

            def tanh_half(tile, m):
                wait(act, z_ps, count(tile, K, m + 1))
                wait(act, gate_done, count(tile, K, m - 1))
                nc.scalar.activation(tanh_z[m % 2][:], ps_z[m % 2][0][:], ACT.Tanh,
                                     scale=half_s1[:, m:m + 1]).then_inc(tanh_done, 1)

            def gelu(tile, m, layer):
                if layer == 1:
                    ps_ready, freed = h1_ps, (2, before(tile))
                    readers, out, s, done, hi_done = (h2_ps, count(before(tile), K)), hb_hi, S_H1, gelu1_done, hb_hi_done
                else:
                    ps_ready, freed = h2_ps, (1, tile)
                    readers, out, s, done, hi_done = (w3_ps, count(before(tile))), hc_hi, S_H2, gelu2_done, hc_hi_done
                s_m = scales[:, s + m:s + m + 1]
                wait(act, ps_ready, count(tile, K, m + 1))
                wait(act, *low_done(*freed, m))
                nc.scalar.activation(h_g[m][:], ps_h[m % 2][:], ACT.Gelu, scale=s_m).then_inc(done, 1)
                wait(act, *readers)
                nc.scalar.activation(out[:, m, :], ps_h[m % 2][:], ACT.Gelu, scale=s_m).then_inc(hi_done, 1)

            def body(tile, attend=True, gated=True):
                ahead2, ahead1 = (tile[0] + 1, tile[1]), after(tile)
                finish = not is_number(tile, 0)
                gelu(tile, 0, 1)
                if finish:
                    ffn_scaled(before(tile))
                if gated and not attend:
                    attn_normed(ahead1)
                gelu(tile, 1, 1)
                if gated and attend:
                    attn_normed(ahead1)
                if attend:
                    xsT_rounded(ahead2)
                gelu(tile, 2, 1)
                gelu(tile, 3, 1)
                if attend:
                    y_rounded(ahead2)
                    gelu(tile, 0, 2)
                    if finish:
                        ffn_normed(before(tile))
                    x2T_rounded(ahead1)
                    gelu(tile, 1, 2)
                    tanh_half(ahead1, 0)
                    tanh_half(ahead1, 1)
                elif gated:
                    x2T_rounded(ahead1)
                    ffn_normed(before(tile))
                    gelu(tile, 0, 2)
                    tanh_half(ahead1, 0)
                    tanh_half(ahead1, 1)
                    gelu(tile, 1, 2)
                else:
                    ffn_normed(before(tile))
                    gelu(tile, 0, 2)
                    gelu(tile, 1, 2)
                gelu(tile, 2, 2)
                if attend:
                    r_rounded(ahead2)
                if gated:
                    tanh_half(ahead1, 2)
                    tanh_half(ahead1, 3)
                gelu(tile, 3, 2)

            def w_rounded(i):
                lo, hi = PIECES[i]
                act.wait_ge(w_in[i], 16)
                nc.scalar.activation(w_hi[:, lo:hi], w_raw[:, lo:hi], ACT.Copy).then_inc(w_hi_done, 1)

            def low_summed(i):
                lo, hi = PIECES[i]
                act.wait_ge(w_lo_done[i], low_parts(i))
                if i > 0:
                    act.wait_ge(lo_sums_done, i)
                nc.scalar.activation(w_abs[:, 0:hi - lo], w_lo[:, lo:hi].bitcast(F32), ACT.Abs,
                                     accum_out=lo_sums[:, i:i + 1]).then_inc(lo_sums_done, 1)

            act.dma_start(table[:], table_dram).then_inc(table_in, 16)
            act.dma_start(scales[:], scales_dram).then_inc(scales_in, 16)
            act.wait_ge(consts_done, 2)
            nc.scalar.activation(warm[:], ones[:], ACT.Gelu)
            act.wait_ge(scales_in, 16)
            nc.scalar.mul(half_s1[:], scales[:, S_1:S_1 + K], 0.5).then_inc(half_s1_done, 1)
            t0, t1 = (0, 0), (0, 1)
            xsT_rounded(t0)
            y_rounded(t0)
            w_rounded(0)
            w_rounded(1)
            w_rounded(2)
            r_rounded(t0)
            xsT_rounded(t1)
            w_rounded(3)
            y_rounded(t1)
            low_summed(0)
            attn_normed(t0)
            low_summed(1)
            x2T_rounded(t0)
            low_summed(2)
            low_summed(3)
            act.wait_ge(half_s1_done, 1)
            tanh_half(t0, 0)
            tanh_half(t0, 1)
            r_rounded(t1)
            tanh_half(t0, 2)
            tanh_half(t0, 3)
            steps(body, act.Fori)
            ffn_scaled(LAST)

        @block.vector
        def _(dve):
            sub, mult, add = ALU.subtract, ALU.mult, ALU.add

            def token_stats(*norms):
                for tile, i, source in norms:
                    for c in range(CHUNKS):
                        last = nc.vector.bn_stats(stats[:, i, c, :], source(c))
                    last.then_inc(ln_stats[i], 1)

            def variances(*norms):
                for tile, i in norms:
                    dve.wait_ge(ln_stats[i], count(tile, 3, 1))
                    by_itself(dve, dve_turns)
                    for c in range(CHUNKS):
                        last = nc.vector.bn_aggr(mean_var[:, i, c, :], stats[:, i, c, :])
                    last.then_inc(ln_stats[i], 1)
                for tile, i in norms:
                    dve.wait_ge(ln_stats[i], count(tile, 3, 2))
                    eps = table[:, C_EPS2:C_EPS2 + 1] if i == 1 else eps_col[:]
                    factor = table[:, C_IGS2:C_IGS2 + 1] if i == 0 else ones[:]
                    nc.vector.tensor_scalar(var_eps[:, i, :], mean_var[:, i, :, 1], eps, factor, add, mult).then_inc(ln_stats[i], 1)

            def layer_stats(*norms):
                token_stats(*norms)
                variances(*[norm[:2] for norm in norms])

            def norm_bias(tile, i):
                wait(dve, ln_rstd[i], count(tile))
                nc.vector.scalar_tensor_tensor(neg_mr[:, i, :], mean_var[:, i, :, 0], -1.0, rstd[:, i, :], mult, mult).then_inc(ln_bias[i], 1)

            def lo_part(out, full, hi, done):
                nc.vector.tensor_tensor(out, full, hi.bitcast(F32), sub).then_inc(done, 1)

            def x_norm(tile):
                q, b = tile
                wait(dve, x_loaded[b], (q + 1) * 16)
                return tile, 0, lambda c: x_in[b][:, c, :]

            def x_stats(tile):
                layer_stats(x_norm(tile))

            def xs_normed(tile):
                b = tile[1]
                wait(dve, ln_rstd[0], count(tile))
                wait(dve, xs_hi_done, count(before(tile)))
                wait(dve, xs_lo_done, count(before(tile)))
                wait(dve, xsT_done, count(before(tile)))
                for c in range(CHUNKS):
                    last = nc.vector.tensor_scalar(xs[:, c, 0:P - 1], x_in[b][:, c, 0:P - 1], mean_var[:, 0, c, 0:1],
                                                   rstd[:, 0, c:c + 1], sub, mult)
                last.then_inc(xs_done, 1)

            def xs_low(tile):
                wait(dve, xs_hi_done, count(tile))
                lo_part(flat(xs_lo), flat(xs), flat(xs_hi), xs_lo_done)

            def xsT_low(tile):
                wait(dve, xsT_hi_done, count(tile))
                lo_part(xsT_lo[:], att_bank(tile, "x")[:], xsT_hi[:], xsT_lo_done)

            def state_chain(tile):
                b = tile[1]
                wait(dve, outer_ps, count(tile))
                wait(dve, state_hi_done, count(before(tile)))
                wait(dve, state_lo_done, count(before(tile)))
                for c in range(CHUNKS - b):
                    out = state[b][:, c + 1, :] if c < CHUNKS - 1 else state[1][:, 0, :]
                    wait(dve, state_done, count_chain(tile, c))
                    nc.vector.scalar_tensor_tensor(out, state[b][:, c, :], G128, att_bank(tile, "outer")[:, chunk(c)], mult, add).then_inc(state_done, 1)

            def state_low(tile):
                wait(dve, state_hi_done, count(tile))
                wait(dve, r_ps, count(before(tile)))
                lo_part(flat(state_lo), flat(state[tile[1]]), flat(state_hi), state_lo_done)

            def y_low(tile):
                wait(dve, y_hi_done, count(tile))
                lo_part(y_lo[:], att_bank(tile, "y")[:], y_hi[:], y_lo_done)

            def scores_masked(tile):
                wait(dve, scores_ps, count(tile))
                wait(dve, scores_hi_done, count(before(tile)))
                wait(dve, scores_lo_done, count(before(tile)))
                tri = table[:, None, C_TRI:C_TRI + P].to_broadcast([P, CHUNKS, P])
                nc.vector.tensor_tensor(scores[:].rearrange("p (c i) -> p c i", c=CHUNKS),
                                        att_bank(tile, "scores")[:].rearrange("p (c i) -> p c i", c=CHUNKS), tri, mult).then_inc(scores_done, 1)

            def scores_low(tile):
                wait(dve, scores_hi_done, count(tile))
                wait(dve, r_ps, count(before(tile)))
                lo_part(scores_lo[:], scores[:], scores_hi[:], scores_lo_done)

            def r_low(tile):
                wait(dve, r_hi_done, count(tile))
                lo_part(r_lo[:], att_bank(tile, "r")[:], r_hi[:], r_lo_done)

            def attn_norm(tile):
                wait(dve, attn_ps, count(tile))
                return tile, 1, lambda c: att_bank(tile, "attn")[:, chunk(c)]

            def attn_stats(tile):
                layer_stats(attn_norm(tile))

            def x1_norm(tile):
                wait(dve, x1_done, count(tile))
                return tile, 2, lambda c: x1[tile[1]][:, c, :]

            def x1_stats(tile):
                layer_stats(x1_norm(tile))

            def x2_normed(tile):
                wait(dve, ln_rstd[2], count(tile))
                wait(dve, x2T_ps, count(before(tile)))
                for c in range(CHUNKS):
                    last = nc.vector.tensor_scalar(x2[:, c, :], x1[tile[1]][:, c, :], mean_var[:, 2, c, 0:1],
                                                   rstd[:, 2, c:c + 1], sub, mult)
                last.then_inc(x2_done, 1)

            def x2T_low(tile):
                wait(dve, x2T_hi_done, count(tile))
                lo_part(x2T_lo[:], ps_att[0][:], x2T_hi[:], x2T_lo_done)

            def silu_gate(tile, m):
                wait(dve, tanh_done, count(tile, K, m + 1))
                wait(dve, silu_done, count(tile, K, m - 1))
                nc.vector.scalar_tensor_tensor(gate[m % 2][:], tanh_z[m % 2][:], 1.0, ps_z[m % 2][0][:], add, mult).then_inc(gate_done, 1)

            def silu_times(tile, m):
                wait(dve, gate_done, count(tile, K, m + 1))
                wait(dve, ha_hi_done, count(tile, K, m - 1))
                wait(dve, ha_lo_done, count(tile, K, m - 1))
                nc.vector.scalar_tensor_tensor(h_a[m % 2][:], gate[m % 2][:], silu_s[:, m:m + 1], ps_z[m % 2][1][:], mult, mult).then_inc(silu_done, 1)

            def ha_low(tile, m):
                wait(dve, ha_hi_done, count(tile, K, m + 1))
                lo_part(ha_lo[:, m, :], h_a[m % 2][:], ha_hi[:, m, :], ha_lo_done)

            def gelu_low(tile, m, layer):
                hi, lo, hi_done, lo_done = ((hb_hi, hb_lo, hb_hi_done, hb_lo_last) if layer == 1
                                            else (hc_hi, hc_lo, hc_hi_done, hc_lo_last))
                wait(dve, hi_done, count(tile, K, m + 1))
                lo_part(lo[:, m, :], h_g[m][:], hi[:, m, :], lo_done)

            def ffn_norm(tile):
                wait(dve, ffn_ps, count(tile))
                return tile, 3, lambda c: ps_z[0][0][:, chunk(c)]

            def ffn_stats(tile):
                layer_stats(ffn_norm(tile))

            def body(tile, attend=True, gated=True):
                ahead2, ahead1 = (tile[0] + 1, tile[1]), after(tile)
                finish = not is_number(tile, 0)
                if attend:
                    layer_stats(attn_norm(ahead1), x_norm(ahead2))
                elif gated:
                    attn_stats(ahead1)
                if attend:
                    xs_normed(ahead2)
                if gated:
                    norm_bias(ahead1, 1)
                if gated and not attend:
                    x1_stats(ahead1)
                if finish:
                    token_stats(ffn_norm(before(tile)))
                if attend:
                    xs_low(ahead2)
                if finish:
                    variances((before(tile), 3))
                if attend:
                    xsT_low(ahead2)
                if attend:
                    x1_stats(ahead1)
                if not gated:
                    norm_bias(before(tile), 3)
                gelu_low(tile, 3, 1)
                if attend:
                    y_low(ahead2)
                if gated:
                    x2_normed(ahead1)
                    if finish:
                        norm_bias(before(tile), 3)
                if attend:
                    state_chain(ahead2)
                if gated:
                    x2T_low(ahead1)
                if attend:
                    scores_masked(ahead2)
                    state_low(ahead2)
                    scores_low(ahead2)
                if gated and attend:
                    silu_gate(ahead1, 0)
                    silu_gate(ahead1, 1)
                    silu_times(ahead1, 0)
                    silu_times(ahead1, 1)
                    ha_low(ahead1, 0)
                    r_low(ahead2)
                    ha_low(ahead1, 1)
                    silu_gate(ahead1, 2)
                    silu_gate(ahead1, 3)
                    silu_times(ahead1, 2)
                    silu_times(ahead1, 3)
                    ha_low(ahead1, 2)
                    ha_low(ahead1, 3)
                elif gated:
                    for m in (0, 2):
                        silu_gate(ahead1, m)
                        silu_times(ahead1, m)
                        silu_gate(ahead1, m + 1)
                        silu_times(ahead1, m + 1)
                        ha_low(ahead1, m)
                        ha_low(ahead1, m + 1)
                gelu_low(tile, 3, 2)

            nc.vector.memset(neg_half[:], -0.5).then_inc(consts_done, 1)
            nc.vector.memset(ones[:], 1.0).then_inc(consts_done, 1)
            nc.vector.memset(eps_col[:], EPS).then_inc(consts_done, 1)
            nc.vector.memset(state[0][:, 0, :], 0.0).then_inc(consts_done, 1)
            t0, t1 = (0, 0), (0, 1)
            dve.wait_ge(table_in, 16)
            for c in range(CHUNKS):
                nc.vector.tensor_copy(xs[:, c, P - 1:P], table[:, C_GS:C_GS + 1]).then_inc(gs_done, 1)
            dve.wait_ge(consts_done, 4)
            x_stats(t0)
            dve.wait_ge(attn_in, 16)
            for w, col, bias in ((wq_aug, A_Q, A_BQ), (wk_aug, A_K, A_BK)):
                nc.vector.tensor_copy(w[:, P - 1:P], attn_w[:, bias:bias + 1]).then_inc(aug_done, 1)
                nc.vector.tensor_scalar(w[:, 0:P - 1], attn_w[:, col:col + P - 1], attn_w[:, col + P - 1:col + P],
                                        None, sub).then_inc(aug_done, 1)
            nc.vector.tensor_scalar(wv_aug[:], attn_w[:, A_V:A_V + P], attn_w[:, A_V + P - 1:A_V + P],
                                    None, sub).then_inc(aug_done, 1)
            dve.wait_ge(gs_done, CHUNKS)
            xs_normed(t0)
            dve.wait_ge(av_ps, 2)
            nc.vector.tensor_copy(a_hi[:], ps_z[1][0][:, 0:P]).then_inc(av_done, 1)
            nc.vector.tensor_copy(v_hi[:], ps_z[1][1][:, 0:P]).then_inc(av_done, 1)
            dve.wait_ge(av_done, 2)
            nc.vector.tensor_tensor(a_lo[:], ps_z[1][0][:, 0:P], a_hi[:].bitcast(F32), sub).then_inc(av_done, 1)
            nc.vector.tensor_tensor(v_lo[:], ps_z[1][1][:, 0:P], v_hi[:].bitcast(F32), sub).then_inc(av_done, 1)
            xsT_low(t0)
            xs_low(t0)
            token_stats(x_norm(t1))
            y_low(t0)
            state_chain(t0)
            variances((t1, 0))
            scores_masked(t0)
            state_low(t0)
            scores_low(t0)
            xs_normed(t1)
            split_low(dve, nc.vector, 2, (0, 1))
            r_low(t0)
            xs_low(t1)
            xsT_low(t1)
            dve.wait_ge(half_s1_done, 1)
            nc.vector.tensor_tensor(silu_s[:], half_s1[:], scales[:, S_2:S_2 + K], mult).then_inc(silu_s_done, 1)
            attn_stats(t0)
            y_low(t1)
            state_chain(t1)
            norm_bias(t0, 1)
            state_low(t1)
            scores_masked(t1)
            split_low(dve, nc.vector, 2, (2,))
            x1_stats(t0)
            scores_low(t1)
            split_low(dve, nc.vector, 2, (3,))
            x2_normed(t0)
            split_low(dve, nc.vector, 3)
            x2T_low(t0)
            dve.wait_ge(silu_s_done, 1)
            silu_gate(t0, 0)
            silu_times(t0, 0)
            silu_gate(t0, 1)
            silu_times(t0, 1)
            dve.wait_ge(lo_sums_done, len(PIECES))
            nc.vector.reduce_sum(lo_sum[:], lo_sums[:], axis=mybir.AxisListType.X).then_inc(lo_sum_done, 1)
            ha_low(t0, 0)
            ha_low(t0, 1)
            silu_gate(t0, 2)
            silu_times(t0, 2)
            r_low(t1)
            dve.wait_ge(flag_ps, 1)
            nc.vector.tensor_copy(flag[0:1, :], ps_h[1][0:1, 0:1]).then_inc(flag_done, 1)
            silu_gate(t0, 3)
            silu_times(t0, 3)
            ha_low(t0, 2)
            ha_low(t0, 3)
            steps(body, dve.Fori)
            ffn_stats(LAST)
            dve.wait_ge(ln_rstd[3], count(LAST))
            dve.wait_ge(result_done, TILES - 1)
            dve.wait_ge(x1_late_done, TILES)
            dve.wait_ge(stored[1], (TILES // 2 - 1) * 16)
            for h in range(2):
                for c in (2 * h, 2 * h + 1):
                    last = nc.vector.tensor_scalar(ffn_n[:, c, :], ps_z[0][0][:, chunk(c)], mean_var[:, 3, c, 0:1],
                                                   rstd[:, 3, c:c + 1], sub, mult)
                last.then_inc(last_n_done, 1)
            for h in range(2):
                part = slice(2 * h, 2 * h + 2)
                dve.wait_ge(last_n_done, h + 1)
                nc.vector.tensor_tensor(result[1][:, part, :], ffn_n[:, part, :], x1_late[:, part, :], add).then_inc(last_result_done, 1)

        @block.tensor
        def _(pe):
            def product(out, left, right, start, stop, exact=False):
                terms = [(0, 0), (0, 1)] if exact else [(0, 0), (0, 1), (1, 0)]
                for n, (i, j) in enumerate(terms):
                    last = nc.tensor.matmul(out, left[i], right[j], start=start and n == 0,
                                            stop=stop and n == len(terms) - 1)
                return last

            def cut(pair, *index):
                return [t[index] for t in pair]

            every = slice(None)

            def transpose4(out, source):
                for c in range(CHUNKS):
                    last = nc.tensor.transpose(out[:, chunk(c)], source(c), table[:, C_IDENT:C_IDENT + P])
                return last

            def xs_transposed(tile):
                wait(pe, xs_done, count(tile))
                if not first_sequence(tile):
                    wait(pe, r_lo_done, count(before(tile)))
                transpose4(att_bank(tile, "x"), lambda c: xs[:, c, :]).then_inc(xsT_done, 1)

            def outer_products(tile):
                wait(pe, xs_lo_done, count(tile))
                if not first_sequence(tile):
                    wait(pe, attn_n_done, count(before(tile)))
                for c in range(CHUNKS - tile[1]):
                    x_c = cut((xs_hi, xs_lo), every, c, every)
                    last = product(att_bank(tile, "outer")[:, chunk(c)], x_c, x_c, True, True)
                last.then_inc(outer_ps, 1)

            def queries(tile):
                wait(pe, xsT_lo_done, count(tile))
                product(att_bank(tile, "y")[:], [a_hi[:], a_lo[:]], [xsT_hi[:], xsT_lo[:]], True, True).then_inc(y_ps, 1)

            def score_blocks(tile):
                wait(pe, y_lo_done, count(tile))
                if not first_sequence(tile):
                    wait(pe, state_done, count_chain(tile))
                for c in range(CHUNKS):
                    last = product(att_bank(tile, "scores")[:, chunk(c)], cut((xsT_hi, xsT_lo), every, chunk(c)),
                                   cut((y_hi, y_lo), every, chunk(c)), True, True)
                last.then_inc(scores_ps, 1)

            def retained(tile, chunks=range(CHUNKS)):
                wait(pe, scores_lo_done, count(tile))
                wait(pe, state_lo_done, count(tile))
                for c in chunks:
                    out = att_bank(tile, "r")[:, chunk(c)]
                    first = tile[1] == 0 and c == 0
                    last = product(out, cut((xs_hi, xs_lo), every, c, every),
                                   cut((scores_hi, scores_lo), every, chunk(c)), True, first)
                    if not first:
                        last = product(out, cut((state_hi, state_lo), every, c, every),
                                       cut((y_hi, y_lo), every, chunk(c)), False, True)
                if c == CHUNKS - 1:
                    last.then_inc(r_ps, 1)

            def values(tile):
                wait(pe, r_lo_done, count(tile))
                if first_sequence(tile):
                    wait(pe, attn_n_done, count(before(tile)))
                for c in range(CHUNKS):
                    last = product(att_bank(tile, "attn")[:, chunk(c)], cut((r_hi, r_lo), every, chunk(c)), [v_hi[:], v_lo[:]], True, True)
                last.then_inc(attn_ps, 1)

            def x2_transposed(tile, behind=True):
                wait(pe, x2_done, count(tile))
                wait(pe, *((y_lo_done, count(after(tile))) if behind else (r_lo_done, count(tile))))
                transpose4(ps_att[0], lambda c: x2[:, c, :]).then_inc(x2T_ps, 1)

            def keep_warm(bank, products):
                for _ in range(products):
                    nc.tensor.matmul(bank[:, 0:P], table[:, C_IDENT:C_IDENT + P], table[:, C_TRI:C_TRI + P], start=True, stop=True)

            def weight(column, m, k=0):
                at = column + k * hidden + m * P
                return [w_hi[:, at:at + P], w_lo[:, at:at + P]]

            def gated_layer(tile, m, exact=False):
                if m == 0:
                    wait(pe, x2T_lo_done, count(tile))
                    wait(pe, ffn_n_done, count((tile[0] - 1, tile[1])))
                wait(pe, silu_done, count(tile, K, m - 1))
                for i, column in enumerate((W_1, W_2)):
                    last = product(ps_z[m % 2][i][:], weight(column, m), [x2T_hi[:], x2T_lo[:]], True, True, exact)
                last.then_inc(z_ps, 1)

            def ffn_parts(exact):
                def hidden_layer(tile, m, layer, ks=range(K)):
                    if layer == 1:
                        parts, column, done = (ha_hi, ha_lo), W_H1, h1_ps
                        freed = (hb_hi_done, tile) if m >= 2 else (hc_hi_done, before(tile))
                    else:
                        parts, column, done = (hb_hi, hb_lo), W_H2, h2_ps
                        freed = (hc_hi_done, tile) if m >= 2 else (hb_hi_done, tile)
                    if layer == 1 and m == 0 and is_number(tile, 0):
                        wait(pe, r_lo_done, 2)
                    if ks[0] == 0:
                        wait(pe, freed[0], count(freed[1], K, (m - 2) % K + 1))
                    for k in ks:
                        if m == 0:
                            wait(pe, *((ha_lo_done, count(tile, K, k + 1)) if layer == 1 else low_done(1, tile, k)))
                        last = product(ps_h[m % 2][:], weight(column, m, k), cut(parts, every, k, every), k == 0, k == K - 1, exact)
                    if ks[-1] == K - 1:
                        last.then_inc(done, 1)

                def last_layer(tile):
                    wait(pe, silu_done, count(after(tile), K, 3) if tile is not LAST else TILES * K)
                    for k in range(K):
                        wait(pe, *low_done(2, tile, k))
                        at = W_3 + k * P
                        last = product(ps_z[0][1][:], [w_hi[:, at:at + P], w_lo[:, at:at + P]],
                                       cut((hc_hi, hc_lo), every, k, every), k == 0, k == K - 1, exact)
                    last.then_inc(w3_ps, 1)

                def ffn_transposed(tile):
                    wait(pe, ffnT_done, count(tile))
                    transpose4(ps_z[0][0], lambda c: ffnT[:, chunk(c)]).then_inc(ffn_ps, 1)

                def body(tile, attend=True, gated=True):
                    ahead2, ahead1 = (tile[0] + 1, tile[1]), after(tile)
                    finish = not is_number(tile, 0)
                    if gated:
                        hidden_layer(tile, 0, 1)
                    else:
                        hidden_layer(tile, 0, 1, range(0, K // 2))
                        keep_warm(ps_att[0], 7)
                        hidden_layer(tile, 0, 1, range(K // 2, K))
                    if finish:
                        last_layer(before(tile))
                    hidden_layer(tile, 1, 1)
                    if not gated:
                        ffn_transposed(before(tile))
                    hidden_layer(tile, 2, 1)
                    if gated and finish:
                        ffn_transposed(before(tile))
                    if attend:
                        xs_transposed(ahead2)
                    hidden_layer(tile, 3, 1)
                    if attend:
                        outer_products(ahead2)
                        queries(ahead2)
                    hidden_layer(tile, 0, 2)
                    if attend:
                        hidden_layer(tile, 1, 2)
                        x2_transposed(ahead1)
                        hidden_layer(tile, 2, 2, range(0, K // 2))
                        score_blocks(ahead2)
                        gated_layer(ahead1, 0, exact)
                        gated_layer(ahead1, 1, exact)
                        hidden_layer(tile, 2, 2, range(K // 2, K))
                        retained(ahead2)
                        gated_layer(ahead1, 2, exact)
                        gated_layer(ahead1, 3, exact)
                        values(ahead2)
                        hidden_layer(tile, 3, 2)
                    elif gated:
                        x2_transposed(ahead1, behind=False)
                        hidden_layer(tile, 1, 2)
                        gated_layer(ahead1, 0, exact)
                        gated_layer(ahead1, 1, exact)
                        hidden_layer(tile, 2, 2)
                        gated_layer(ahead1, 2, exact)
                        gated_layer(ahead1, 3, exact)
                        hidden_layer(tile, 3, 2)
                    else:
                        for m in range(1, K):
                            hidden_layer(tile, m, 2)

                steps(body, pe.Fori)
                last_layer(LAST)
                ffn_transposed(LAST)

            pe.wait_ge(table_in, 16)
            keep_warm(ps_h[0], 6)
            pe.wait_ge(aug_done, 5)
            nc.tensor.matmul(ps_z[1][0][:, 0:P], wq_aug[:], wk_aug[:], start=True, stop=True).then_inc(av_ps, 1)
            nc.tensor.transpose(ps_z[1][1][:, 0:P], wv_aug[:], table[:, C_IDENT:C_IDENT + P]).then_inc(av_ps, 1)
            t0, t1 = (0, 0), (0, 1)
            keep_warm(ps_h[0], 2)
            xs_transposed(t0)
            keep_warm(ps_h[0], 6)
            pe.wait_ge(av_done, 4)
            queries(t0)
            outer_products(t0)
            score_blocks(t0)
            keep_warm(ps_h[0], 10)
            retained(t0)
            xs_transposed(t1)
            keep_warm(ps_h[1], 5)
            values(t0)
            queries(t1)
            outer_products(t1)
            score_blocks(t1)
            keep_warm(ps_z[0][0], 23)
            retained(t1, (0, 1))
            keep_warm(ps_z[0][0], 1)
            x2_transposed(t0, behind=False)
            retained(t1, (2,))
            gated_layer(t0, 0)
            gated_layer(t0, 1)
            retained(t1, (3,))
            gated_layer(t0, 2)
            pe.wait_ge(lo_sum_done, 1)
            nc.tensor.matmul(ps_h[1][0:1, 0:1], lo_sum[:], ones[:], start=True, stop=True).then_inc(flag_ps, 1)
            gated_layer(t0, 3)
            keep_warm(ps_att[0], 8)
            values(t1)
            pe.wait_ge(flag_done, 1)
            any_lo = pe.value_load(flag[0:1, 0:1].bitcast(I32))
            with pe.If(any_lo != 0):
                ffn_parts(exact=False)
            with pe.Else():
                ffn_parts(exact=True)


def kernel(**inputs):
    import concourse.bacc as _bacc
    from concourse.bass_utils import run_bass_kernel_spmd as _run

    a = {name.removeprefix("L0_"): np.asarray(value) for name, value in inputs.items()}
    batch, seq, d = a["attn_x"].shape
    hidden = a["ffn_w1_w"].shape[0]
    k = hidden // P

    def by_input(w):
        return w.T.reshape(-1, P, w.shape[0]).transpose(1, 0, 2).reshape(P, -1)

    def by_partition(s):
        return s.reshape(-1, P).T

    arrays = {
        "x": a["attn_x"].reshape(batch * seq, d),
        "table": decay_tables(),
        "attn_w": np.concatenate([a["attn_Wq"], a["attn_Wk"], a["attn_Wv"], a["attn_bq"][:, None], a["attn_bk"][:, None]], axis=1),
        "ffn_w": np.concatenate([by_input(a[f"ffn_{n}_w"]) for n in ("w1", "w2", "h1", "h2", "w3")], axis=1),
        "scales": np.concatenate([by_partition(a[f"ffn_{n}_s"]) for n in ("w1", "w2", "h1", "h2", "w3")], axis=1),
    }
    arrays = {f"in_{n}": np.ascontiguousarray(v) for n, v in arrays.items()}
    nc = _bacc.Bacc("TRN2", target_bir_lowering=False, num_devices=1)
    args = [nc.dram_tensor(n, v.shape, F32, kind="ExternalInput").ap() for n, v in arrays.items()]
    out = nc.dram_tensor("out_0", (batch * seq, d), F32, kind="ExternalOutput").ap()
    sandwich(nc, *args, out, hidden)
    r = _run(nc, [arrays], core_ids=[0])
    return r.results[0]["out_0"].reshape(batch, seq, d)
```

```python
from contextlib import ExitStack

import numpy as np

import concourse.bass as bass
from concourse import mybir

F32 = mybir.dt.float32
F32R = mybir.dt.float32r
I32 = mybir.dt.int32
ALU = mybir.AluOpType
ACT = mybir.ActivationFunctionType

P = 128
EPS = 1e-5
GAMMA = 0.96875
CHUNKS = 4
TOK = CHUNKS * P

C_IDENT, C_TRI, C_GS, C_IGS2, C_EPS2 = 0, P, 2 * P, 2 * P + 1, 2 * P + 2
C_COLS = 2 * P + 3
A_Q, A_K, A_V, A_BQ, A_BK = 0, P, 2 * P, 3 * P, 3 * P + 1
A_COLS = 3 * P + 2


def decay_tables():
    j = np.arange(P, dtype=np.float64)
    gs = GAMMA ** ((P - 1 - j) / 2)
    table = np.zeros((P, C_COLS), np.float64)
    table[:, C_IDENT:C_IDENT + P] = np.eye(P)
    table[:, C_TRI:C_TRI + P] = (j[:, None] <= j[None, :]) * GAMMA ** -float(P)
    table[:, C_GS] = gs
    table[:, C_IGS2] = gs ** -2.0
    table[:, C_EPS2] = EPS * (gs / GAMMA ** (j + 1)) ** 2
    return table.astype(np.float32)


def sandwich(nc, x_dram, table_dram, attn_w_dram, ffn_w_dram, scales_dram, out_dram, hidden):
    K = hidden // P
    TILES = x_dram.shape[0] // TOK
    G128 = GAMMA ** float(P)

    W_1, W_2 = 0, hidden
    W_H1 = 2 * hidden
    W_H2 = W_H1 + K * hidden
    W_3 = W_H2 + K * hidden
    W_COLS = W_3 + K * P
    S_1, S_2, S_H1, S_H2, S_3 = 0, K, 2 * K, 3 * K, 4 * K
    S_COLS = 4 * K + 1
    PIECES = [(W_1, W_H1), (W_H1, W_H2), (W_H2, W_3), (W_3, W_COLS)]

    x_tiles = x_dram.rearrange("(t c p) h -> t p c h", c=CHUNKS, p=P)
    out_tiles = out_dram.rearrange("(t c p) h -> t p c h", c=CHUNKS, p=P)

    with ExitStack() as ctx:
        def sb(name, shape, dt=F32):
            return ctx.enter_context(nc.sbuf_tensor(name, shape, dt))

        def sem(name):
            return ctx.enter_context(nc.semaphore(name))

        def bank(name):
            return ctx.enter_context(nc.psum_tensor(name, [P, TOK], F32))

        def split(name, shape):
            return sb(name + "_hi", shape, F32R), sb(name + "_lo", shape, F32R)

        table = sb("table", [P, C_COLS])
        attn_w = sb("attn_w", [P, A_COLS])
        scales = sb("scales", [P, S_COLS])
        w_raw = sb("w_raw", [P, W_COLS])
        w_hi, w_lo = split("w", [P, W_COLS])
        w_abs = sb("w_abs", [P, K * hidden])
        lo_sums = sb("lo_sums", [P, len(PIECES)])
        lo_sum = sb("lo_sum", [P, 1])
        warm = sb("warm", [P, 1])
        eps_col = sb("eps_col", [P, 1])
        flag = sb("flag", [P, 1])
        ones = sb("ones", [P, 1])
        half_s1 = sb("half_s1", [P, K])
        silu_s = sb("silu_s", [P, K])
        neg_half = sb("neg_half", [P, CHUNKS])
        wq_aug = sb("wq_aug", [P, P])
        wk_aug = sb("wk_aug", [P, P])
        wv_aug = sb("wv_aug", [P, P])
        a_hi, a_lo = split("a", [P, P])
        v_hi, v_lo = split("v", [P, P])

        x_in = [sb(f"x_in{b}", [P, CHUNKS, P]) for b in range(2)]
        xs = sb("xs", [P, CHUNKS, P])
        xs_hi, xs_lo = split("xs", [P, CHUNKS, P])
        xsT_hi, xsT_lo = split("xsT", [P, TOK])
        y_hi, y_lo = split("y", [P, TOK])
        state = [sb(f"state{b}", [P, CHUNKS, P]) for b in range(2)]
        state_hi, state_lo = split("state", [P, CHUNKS, P])
        scores = sb("scores", [P, TOK])
        scores_hi, scores_lo = split("scores", [P, TOK])
        r_hi, r_lo = split("r", [P, TOK])
        attn_n = sb("attn_n", [P, CHUNKS, P])
        x1 = [sb(f"x1_{b}", [P, CHUNKS, P]) for b in range(2)]
        x1_late = sb("x1_late", [P, CHUNKS, P])
        x2 = sb("x2", [P, CHUNKS, P])
        x2T_hi, x2T_lo = split("x2T", [P, TOK])
        tanh_z = [sb(f"tanh_z{i}", [P, TOK]) for i in range(2)]
        gate = [sb(f"gate{i}", [P, TOK]) for i in range(2)]
        h_a = [sb(f"h_a{i}", [P, TOK]) for i in range(2)]
        h_g = [sb(f"h_g{m}", [P, TOK]) for m in range(K)]
        ha_hi, ha_lo = split("ha", [P, K, TOK])
        hb_hi, hb_lo = split("hb", [P, K, TOK])
        hc_hi, hc_lo = split("hc", [P, K, TOK])
        ffnT = sb("ffnT", [P, TOK])
        ffn_n = sb("ffn_n", [P, CHUNKS, P])
        result = [sb(f"result{b}", [P, CHUNKS, P]) for b in range(2)]
        stats = sb("stats", [P, 4, CHUNKS, 6])
        mean_var = sb("mean_var", [P, 4, CHUNKS, 2])
        var_eps = sb("var_eps", [P, 4, CHUNKS])
        rstd = sb("rstd", [P, 4, CHUNKS])
        neg_mr = sb("neg_mr", [P, 4, CHUNKS])

        ps_att = [bank(f"ps_att{i}") for i in range(2)]
        ps_h = [bank(f"ps_h{i}") for i in range(2)]
        ps_z = [[bank(f"ps_z{p}{i}") for i in range(2)] for p in range(2)]

        table_in, attn_in, scales_in = sem("table_in"), sem("attn_in"), sem("scales_in")
        w_in = [sem(f"w_in{i}") for i in range(len(PIECES))]
        x_loaded = [sem(f"x_loaded{b}") for b in range(2)]
        stored = [sem(f"stored{b}") for b in range(2)]
        consts_done, aug_done, gs_done = sem("consts_done"), sem("aug_done"), sem("gs_done")
        av_ps, av_done = sem("av_ps"), sem("av_done")
        half_s1_done, silu_s_done = sem("half_s1_done"), sem("silu_s_done")
        lo_sums_done, lo_sum_done, flag_ps, flag_done = sem("lo_sums_done"), sem("lo_sum_done"), sem("flag_ps"), sem("flag_done")
        w_hi_done = sem("w_hi_done")
        w_lo_done = [sem(f"w_lo_done{i}") for i in range(len(PIECES))]
        ln_stats = [sem(f"ln{i}_stats") for i in range(4)]
        ln_rstd = [sem(f"ln{i}_rstd") for i in range(4)]
        ln_bias = {i: sem(f"ln{i}_bias") for i in (1, 3)}
        xs_done, xs_hi_done, xs_lo_done = sem("xs_done"), sem("xs_hi_done"), sem("xs_lo_done")
        xsT_done, xsT_hi_done, xsT_lo_done = sem("xsT_done"), sem("xsT_hi_done"), sem("xsT_lo_done")
        y_ps, y_hi_done, y_lo_done = sem("y_ps"), sem("y_hi_done"), sem("y_lo_done")
        outer_ps, state_done = sem("outer_ps"), sem("state_done")
        state_hi_done, state_lo_done = sem("state_hi_done"), sem("state_lo_done")
        scores_ps, scores_done = sem("scores_ps"), sem("scores_done")
        scores_hi_done, scores_lo_done = sem("scores_hi_done"), sem("scores_lo_done")
        r_ps, r_hi_done, r_lo_done = sem("r_ps"), sem("r_hi_done"), sem("r_lo_done")
        attn_ps, attn_n_done, x1_done, x1_late_done = sem("attn_ps"), sem("attn_n_done"), sem("x1_done"), sem("x1_late_done")
        x2_done, x2T_ps, x2T_hi_done, x2T_lo_done = sem("x2_done"), sem("x2T_ps"), sem("x2T_hi_done"), sem("x2T_lo_done")
        z_ps, tanh_done, gate_done, silu_done = sem("z_ps"), sem("tanh_done"), sem("gate_done"), sem("silu_done")
        ha_hi_done, ha_lo_done = sem("ha_hi_done"), sem("ha_lo_done")
        h1_ps, gelu1_done, hb_hi_done, hb_lo_done = sem("h1_ps"), sem("gelu1_done"), sem("hb_hi_done"), sem("hb_lo_done")
        h2_ps, gelu2_done, hc_hi_done, hc_lo_done = sem("h2_ps"), sem("gelu2_done"), sem("hc_hi_done"), sem("hc_lo_done")
        hb_lo_last, hc_lo_last = sem("hb_lo_last"), sem("hc_lo_last")
        w3_ps, ffnT_done, ffn_ps, ffn_n_done, result_done = sem("w3_ps"), sem("ffnT_done"), sem("ffn_ps"), sem("ffn_n_done"), sem("result_done")

        last_n_done, last_result_done = sem("last_n_done"), sem("last_result_done")

        pool_turns, dve_turns = sem("pool_turns"), sem("dve_turns")

        def after(tile):
            q, b = tile
            return (q, 1) if b == 0 else (q + 1, 0)

        def before(tile):
            q, b = tile
            return (q - 1, 1) if b == 0 else (q, 0)

        def count(tile, per=1, upto=None):
            q, b = tile
            return q * (2 * per) + (b * per + (per if upto is None else upto))

        LAST = (TILES // 2 - 1, 1)

        STEADY_BANKS = dict(x=ps_att[0], y=ps_att[0], outer=ps_att[1], scores=ps_att[1], r=ps_att[0], attn=ps_att[1])
        FIRST_BANKS = [dict(x=ps_att[0], y=ps_h[1], outer=ps_z[0][0], scores=ps_z[1][0], r=ps_att[0], attn=ps_att[1]),
                       dict(x=ps_h[0], y=ps_h[1], outer=ps_z[0][1], scores=ps_z[1][1], r=ps_h[0], attn=ps_att[1])]

        def count_chain(tile, upto=None):
            q, b = tile
            return q * (2 * CHUNKS - 1) + (b * CHUNKS + (CHUNKS - b if upto is None else upto))

        def is_number(tile, number):
            return isinstance(tile[0], int) and tile[0] * 2 + tile[1] == number

        def first_sequence(tile):
            return isinstance(tile[0], int) and tile[0] == 0

        def att_bank(tile, stage):
            return (FIRST_BANKS[tile[1]] if first_sequence(tile) else STEADY_BANKS)[stage]

        def low_done(layer, tile, m):
            by_pool, by_dve = (hb_lo_done, hb_lo_last) if layer == 1 else (hc_lo_done, hc_lo_last)
            return (by_dve, count(tile)) if m == K - 1 else (by_pool, count(tile, K - 1, m + 1))

        def wait(eng, semaphore, value):
            if not isinstance(value, int) or value > 0:
                eng.wait_ge(semaphore, value)

        def by_itself(eng, turns):
            eng.sem_inc(turns, 1)

        def steps(body, without_attention, last_body, fori):
            body((0, 0))
            body((0, 1))
            with fori(1, TILES // 2 - 1) as q:
                body((q, 0))
                body((q, 1))
            without_attention(before(LAST))
            last_body(LAST)

        def chunk(c):
            return slice(c * P, (c + 1) * P)

        def flat(t):
            return t[:].rearrange("p c h -> p (c h)")

        def low_parts(i):
            return (PIECES[i][1] - PIECES[i][0]) // TOK

        def split_low(eng, ops, i, parts=None):
            eng.wait_ge(w_hi_done, i + 1)
            for part in range(low_parts(i)) if parts is None else parts:
                at = PIECES[i][0] + part * TOK
                ops.tensor_tensor(w_lo[:, at:at + TOK], w_raw[:, at:at + TOK], w_hi[:, at:at + TOK].bitcast(F32), ALU.subtract).then_inc(w_lo_done[i], 1)

        block = ctx.enter_context(nc.Block())

        @block.sync
        def _(sp):
            def load(tile, q):
                wait(sp, x1_done, count((q - 1, tile)))
                sp.dma_start(x_in[tile][:], x_tiles[q * 2 + tile]).then_inc(x_loaded[tile], 16)

            def store(b, q):
                wait(sp, result_done, count((q, b)))
                sp.dma_start(out_tiles[q * 2 + b], result[b][:]).then_inc(stored[b], 16)

            load(0, 0)
            sp.dma_start(attn_w[:], attn_w_dram).then_inc(attn_in, 16)
            load(1, 0)
            for i, (lo, hi) in enumerate(PIECES):
                sp.dma_start(w_raw[:, lo:hi], ffn_w_dram[:, lo:hi]).then_inc(w_in[i], 16)
            load(0, 1)
            load(1, 1)
            with sp.Fori(2, TILES // 2) as q:
                load(0, q)
                store(0, q - 2)
                load(1, q)
                store(1, q - 2)
            store(0, TILES // 2 - 2)
            store(1, TILES // 2 - 2)
            store(0, TILES // 2 - 1)
            for h in range(2):
                part = slice(2 * h, 2 * h + 2)
                sp.wait_ge(last_result_done, h + 1)
                sp.dma_start(out_tiles[TILES - 1][:, part, :], result[1][:, part, :]).then_inc(stored[1], 16)
            sp.wait_ge(stored[0], 16 * (TILES // 2))
            sp.wait_ge(stored[1], 16 * (TILES // 2 + 1))

        @block.gpsimd
        def _(pool):
            def inverse_root(tile, i):
                wait(pool, ln_stats[i], count(tile, 3))
                nc.gpsimd.tensor_tensor(rstd[:, i, :], var_eps[:, i, :], neg_half[:], ALU.pow).then_inc(ln_rstd[i], 1)

            def round_hi(out, in_, done):
                by_itself(pool, pool_turns)
                nc.gpsimd.tensor_scalar(out, in_, 1.0, 1.0, ALU.mult, ALU.mult).then_inc(done, 1)

            def xs_rounded(tile):
                wait(pool, xs_done, count(tile))
                wait(pool, r_ps, count(before(tile)))
                round_hi(flat(xs_hi), flat(xs), xs_hi_done)

            def state_rounded(tile):
                wait(pool, state_done, count_chain(tile))
                wait(pool, r_ps, count(before(tile)))
                round_hi(flat(state_hi), flat(state[tile[1]]), state_hi_done)

            def scores_rounded(tile):
                wait(pool, scores_done, count(tile))
                wait(pool, r_ps, count(before(tile)))
                round_hi(scores_hi[:], scores[:], scores_hi_done)

            def silu_rounded(tile, m):
                wait(pool, silu_done, count(tile, K, m + 1))
                wait(pool, h1_ps, count(before(tile), K))
                round_hi(ha_hi[:, m, :], h_a[m % 2][:], ha_hi_done)

            def gelu_low(tile, m, layer):
                hi, lo, hi_done, lo_done = ((hb_hi, hb_lo, hb_hi_done, hb_lo_done) if layer == 1
                                            else (hc_hi, hc_lo, hc_hi_done, hc_lo_done))
                wait(pool, hi_done, count(tile, K, m + 1))
                nc.gpsimd.tensor_tensor(lo[:, m, :], h_g[m][:], hi[:, m, :].bitcast(F32), ALU.subtract).then_inc(lo_done, 1)

            def residual1(tile):
                b = tile[1]
                wait(pool, attn_n_done, count(tile))
                wait(pool, x1_late_done, count((tile[0] - 1, b)))
                nc.gpsimd.tensor_tensor(x1[b][:], attn_n[:], x_in[b][:], ALU.add).then_inc(x1_done, 1)

            def keep_x1(tile):
                wait(pool, result_done, count(before(tile)))
                by_itself(pool, pool_turns)
                nc.gpsimd.tensor_scalar(flat(x1_late), flat(x1[tile[1]]), 1.0, 1.0, ALU.mult, ALU.mult).then_inc(x1_late_done, 1)

            def residual2(tile):
                q, b = tile
                wait(pool, ffn_n_done, count(tile))
                wait(pool, x1_late_done, count(tile))
                if not isinstance(q, int) or q > 0:
                    wait(pool, stored[b], q * 16)
                nc.gpsimd.tensor_tensor(result[b][:], ffn_n[:], x1_late[:], ALU.add).then_inc(result_done, 1)

            def body(tile):
                ahead2, ahead1, behind = after(after(tile)), after(tile), before(tile)
                finish = not is_number(tile, 0)
                inverse_root(ahead2, 0)
                inverse_root(ahead1, 1)
                gelu_low(tile, 0, 1)
                xs_rounded(ahead2)
                residual1(ahead1)
                gelu_low(tile, 1, 1)
                gelu_low(tile, 2, 1)
                inverse_root(ahead1, 2)
                if finish:
                    inverse_root(behind, 3)
                gelu_low(tile, 0, 2)
                state_rounded(ahead2)
                scores_rounded(ahead2)
                gelu_low(tile, 1, 2)
                silu_rounded(ahead1, 0)
                silu_rounded(ahead1, 1)
                if finish:
                    residual2(behind)
                keep_x1(tile)
                gelu_low(tile, 2, 2)
                silu_rounded(ahead1, 2)
                silu_rounded(ahead1, 3)

            def without_attention(tile):
                ahead1, behind = after(tile), before(tile)
                inverse_root(ahead1, 1)
                gelu_low(tile, 0, 1)
                residual1(ahead1)
                gelu_low(tile, 1, 1)
                gelu_low(tile, 2, 1)
                inverse_root(ahead1, 2)
                inverse_root(behind, 3)
                gelu_low(tile, 0, 2)
                gelu_low(tile, 1, 2)
                silu_rounded(ahead1, 0)
                silu_rounded(ahead1, 1)
                residual2(behind)
                silu_rounded(ahead1, 2)
                silu_rounded(ahead1, 3)
                gelu_low(tile, 2, 2)
                keep_x1(tile)

            def last_body(tile):
                gelu_low(tile, 0, 1)
                gelu_low(tile, 1, 1)
                inverse_root(before(tile), 3)
                gelu_low(tile, 2, 1)
                gelu_low(tile, 0, 2)
                gelu_low(tile, 1, 2)
                gelu_low(tile, 2, 2)
                residual2(before(tile))
                keep_x1(tile)

            pool.wait_ge(consts_done, 1)
            t0, t1 = (0, 0), (0, 1)
            inverse_root(t0, 0)
            xs_rounded(t0)
            state_rounded(t0)
            scores_rounded(t0)
            inverse_root(t1, 0)
            split_low(pool, nc.gpsimd, 0)
            split_low(pool, nc.gpsimd, 1, (0,))
            xs_rounded(t1)
            split_low(pool, nc.gpsimd, 1, (1, 2))
            inverse_root(t0, 1)
            state_rounded(t1)
            residual1(t0)
            scores_rounded(t1)
            split_low(pool, nc.gpsimd, 1, (3,))
            inverse_root(t0, 2)
            for m in range(K):
                silu_rounded(t0, m)
            steps(body, without_attention, last_body, pool.Fori)
            inverse_root(LAST, 3)

        @block.scalar
        def _(act):
            def xsT_rounded(tile):
                wait(act, xsT_done, count(tile))
                wait(act, scores_ps, count(before(tile)))
                nc.scalar.activation(xsT_hi[:], att_bank(tile, "x")[:], ACT.Copy).then_inc(xsT_hi_done, 1)

            def y_rounded(tile):
                wait(act, y_ps, count(tile))
                wait(act, r_ps, count(before(tile)))
                nc.scalar.activation(y_hi[:], att_bank(tile, "y")[:], ACT.Copy).then_inc(y_hi_done, 1)

            def r_rounded(tile):
                wait(act, r_ps, count(tile))
                wait(act, attn_ps, count(before(tile)))
                nc.scalar.activation(r_hi[:], att_bank(tile, "r")[:], ACT.Copy).then_inc(r_hi_done, 1)

            def x2T_rounded(tile):
                wait(act, x2T_ps, count(tile))
                wait(act, z_ps, count(before(tile), K))
                nc.scalar.activation(x2T_hi[:], ps_att[0][:], ACT.Copy).then_inc(x2T_hi_done, 1)

            def normalise(i, source, out, done):
                for c in range(CHUNKS):
                    last = nc.scalar.activation(out[:, c, :], source[:, chunk(c)], ACT.Identity,
                                                bias=neg_mr[:, i, c:c + 1], scale=rstd[:, i, c:c + 1])
                last.then_inc(done, 1)

            def attn_normed(tile):
                wait(act, ln_bias[1], count(tile))
                wait(act, x1_done, count(before(tile)))
                normalise(1, att_bank(tile, "attn"), attn_n, attn_n_done)

            def ffn_scaled(tile):
                wait(act, w3_ps, count(tile))
                wait(act, ffn_ps, count(before(tile)))
                nc.scalar.activation(ffnT[:], ps_z[0][1][:], ACT.Identity, scale=scales[:, S_3:S_3 + 1]).then_inc(ffnT_done, 1)

            def ffn_normed(tile):
                wait(act, ln_bias[3], count(tile))
                wait(act, result_done, count(before(tile)))
                normalise(3, ps_z[0][0], ffn_n, ffn_n_done)

            def tanh_half(tile, m):
                wait(act, z_ps, count(tile, K, m + 1))
                wait(act, gate_done, count(tile, K, m - 1))
                nc.scalar.activation(tanh_z[m % 2][:], ps_z[m % 2][0][:], ACT.Tanh,
                                     scale=half_s1[:, m:m + 1]).then_inc(tanh_done, 1)

            def gelu(tile, m, layer):
                if layer == 1:
                    ps_ready, freed = h1_ps, (2, before(tile))
                    readers, out, s, done, hi_done = (h2_ps, count(before(tile), K)), hb_hi, S_H1, gelu1_done, hb_hi_done
                else:
                    ps_ready, freed = h2_ps, (1, tile)
                    readers, out, s, done, hi_done = (w3_ps, count(before(tile))), hc_hi, S_H2, gelu2_done, hc_hi_done
                s_m = scales[:, s + m:s + m + 1]
                wait(act, ps_ready, count(tile, K, m + 1))
                wait(act, *low_done(*freed, m))
                nc.scalar.activation(h_g[m][:], ps_h[m % 2][:], ACT.Gelu, scale=s_m).then_inc(done, 1)
                wait(act, *readers)
                nc.scalar.activation(out[:, m, :], ps_h[m % 2][:], ACT.Gelu, scale=s_m).then_inc(hi_done, 1)

            def body(tile):
                ahead2, ahead1, behind = after(after(tile)), after(tile), before(tile)
                finish = not is_number(tile, 0)
                gelu(tile, 0, 1)
                if finish:
                    ffn_scaled(behind)
                gelu(tile, 1, 1)
                attn_normed(ahead1)
                xsT_rounded(ahead2)
                gelu(tile, 2, 1)
                gelu(tile, 3, 1)
                y_rounded(ahead2)
                gelu(tile, 0, 2)
                if finish:
                    ffn_normed(behind)
                x2T_rounded(ahead1)
                gelu(tile, 1, 2)
                tanh_half(ahead1, 0)
                tanh_half(ahead1, 1)
                gelu(tile, 2, 2)
                r_rounded(ahead2)
                tanh_half(ahead1, 2)
                tanh_half(ahead1, 3)
                gelu(tile, 3, 2)

            def without_attention(tile):
                ahead1, behind = after(tile), before(tile)
                gelu(tile, 0, 1)
                ffn_scaled(behind)
                attn_normed(ahead1)
                gelu(tile, 1, 1)
                gelu(tile, 2, 1)
                gelu(tile, 3, 1)
                x2T_rounded(ahead1)
                ffn_normed(behind)
                gelu(tile, 0, 2)
                tanh_half(ahead1, 0)
                tanh_half(ahead1, 1)
                gelu(tile, 1, 2)
                gelu(tile, 2, 2)
                tanh_half(ahead1, 2)
                tanh_half(ahead1, 3)
                gelu(tile, 3, 2)

            def last_body(tile):
                gelu(tile, 0, 1)
                ffn_scaled(before(tile))
                for m in range(1, K):
                    gelu(tile, m, 1)
                ffn_normed(before(tile))
                for m in range(K):
                    gelu(tile, m, 2)

            def w_rounded(i):
                lo, hi = PIECES[i]
                act.wait_ge(w_in[i], 16)
                nc.scalar.activation(w_hi[:, lo:hi], w_raw[:, lo:hi], ACT.Copy).then_inc(w_hi_done, 1)

            def low_summed(i):
                lo, hi = PIECES[i]
                act.wait_ge(w_lo_done[i], low_parts(i))
                if i > 0:
                    act.wait_ge(lo_sums_done, i)
                nc.scalar.activation(w_abs[:, 0:hi - lo], w_lo[:, lo:hi].bitcast(F32), ACT.Abs,
                                     accum_out=lo_sums[:, i:i + 1]).then_inc(lo_sums_done, 1)

            act.dma_start(table[:], table_dram).then_inc(table_in, 16)
            act.dma_start(scales[:], scales_dram).then_inc(scales_in, 16)
            act.wait_ge(consts_done, 2)
            nc.scalar.activation(warm[:], ones[:], ACT.Gelu)
            act.wait_ge(scales_in, 16)
            nc.scalar.mul(half_s1[:], scales[:, S_1:S_1 + K], 0.5).then_inc(half_s1_done, 1)
            t0, t1 = (0, 0), (0, 1)
            xsT_rounded(t0)
            y_rounded(t0)
            w_rounded(0)
            w_rounded(1)
            w_rounded(2)
            r_rounded(t0)
            xsT_rounded(t1)
            w_rounded(3)
            y_rounded(t1)
            low_summed(0)
            attn_normed(t0)
            low_summed(1)
            x2T_rounded(t0)
            low_summed(2)
            low_summed(3)
            act.wait_ge(half_s1_done, 1)
            tanh_half(t0, 0)
            tanh_half(t0, 1)
            r_rounded(t1)
            tanh_half(t0, 2)
            tanh_half(t0, 3)
            steps(body, without_attention, last_body, act.Fori)
            ffn_scaled(LAST)

        @block.vector
        def _(dve):
            sub, mult, add = ALU.subtract, ALU.mult, ALU.add

            def token_stats(*norms):
                for tile, i, source in norms:
                    for c in range(CHUNKS):
                        last = nc.vector.bn_stats(stats[:, i, c, :], source(c))
                    last.then_inc(ln_stats[i], 1)

            def variances(*norms):
                for tile, i in norms:
                    dve.wait_ge(ln_stats[i], count(tile, 3, 1))
                    by_itself(dve, dve_turns)
                    for c in range(CHUNKS):
                        last = nc.vector.bn_aggr(mean_var[:, i, c, :], stats[:, i, c, :])
                    last.then_inc(ln_stats[i], 1)
                for tile, i in norms:
                    dve.wait_ge(ln_stats[i], count(tile, 3, 2))
                    eps = table[:, C_EPS2:C_EPS2 + 1] if i == 1 else eps_col[:]
                    factor = table[:, C_IGS2:C_IGS2 + 1] if i == 0 else ones[:]
                    nc.vector.tensor_scalar(var_eps[:, i, :], mean_var[:, i, :, 1], eps, factor, add, mult).then_inc(ln_stats[i], 1)

            def layer_stats(*norms):
                token_stats(*norms)
                variances(*[norm[:2] for norm in norms])

            def norm_bias(tile, i):
                wait(dve, ln_rstd[i], count(tile))
                nc.vector.scalar_tensor_tensor(neg_mr[:, i, :], mean_var[:, i, :, 0], -1.0, rstd[:, i, :], mult, mult).then_inc(ln_bias[i], 1)

            def lo_part(out, full, hi, done):
                nc.vector.tensor_tensor(out, full, hi.bitcast(F32), sub).then_inc(done, 1)

            def x_norm(tile):
                q, b = tile
                wait(dve, x_loaded[b], (q + 1) * 16)
                return tile, 0, lambda c: x_in[b][:, c, :]

            def xs_normed(tile):
                b = tile[1]
                wait(dve, ln_rstd[0], count(tile))
                wait(dve, xs_hi_done, count(before(tile)))
                wait(dve, xs_lo_done, count(before(tile)))
                wait(dve, xsT_done, count(before(tile)))
                for c in range(CHUNKS):
                    last = nc.vector.tensor_scalar(xs[:, c, 0:P - 1], x_in[b][:, c, 0:P - 1], mean_var[:, 0, c, 0:1],
                                                   rstd[:, 0, c:c + 1], sub, mult)
                last.then_inc(xs_done, 1)

            def xs_low(tile):
                wait(dve, xs_hi_done, count(tile))
                lo_part(flat(xs_lo), flat(xs), flat(xs_hi), xs_lo_done)

            def xsT_low(tile):
                wait(dve, xsT_hi_done, count(tile))
                lo_part(xsT_lo[:], att_bank(tile, "x")[:], xsT_hi[:], xsT_lo_done)

            def state_chain(tile):
                b = tile[1]
                wait(dve, outer_ps, count(tile))
                wait(dve, state_hi_done, count(before(tile)))
                wait(dve, state_lo_done, count(before(tile)))
                for c in range(CHUNKS - b):
                    out = state[b][:, c + 1, :] if c < CHUNKS - 1 else state[1][:, 0, :]
                    wait(dve, state_done, count_chain(tile, c))
                    nc.vector.scalar_tensor_tensor(out, state[b][:, c, :], G128, att_bank(tile, "outer")[:, chunk(c)], mult, add).then_inc(state_done, 1)

            def state_low(tile):
                wait(dve, state_hi_done, count(tile))
                wait(dve, r_ps, count(before(tile)))
                lo_part(flat(state_lo), flat(state[tile[1]]), flat(state_hi), state_lo_done)

            def y_low(tile):
                wait(dve, y_hi_done, count(tile))
                lo_part(y_lo[:], att_bank(tile, "y")[:], y_hi[:], y_lo_done)

            def scores_masked(tile):
                wait(dve, scores_ps, count(tile))
                wait(dve, scores_hi_done, count(before(tile)))
                wait(dve, scores_lo_done, count(before(tile)))
                tri = table[:, None, C_TRI:C_TRI + P].to_broadcast([P, CHUNKS, P])
                nc.vector.tensor_tensor(scores[:].rearrange("p (c i) -> p c i", c=CHUNKS),
                                        att_bank(tile, "scores")[:].rearrange("p (c i) -> p c i", c=CHUNKS), tri, mult).then_inc(scores_done, 1)

            def scores_low(tile):
                wait(dve, scores_hi_done, count(tile))
                wait(dve, r_ps, count(before(tile)))
                lo_part(scores_lo[:], scores[:], scores_hi[:], scores_lo_done)

            def r_low(tile):
                wait(dve, r_hi_done, count(tile))
                lo_part(r_lo[:], att_bank(tile, "r")[:], r_hi[:], r_lo_done)

            def attn_norm(tile):
                wait(dve, attn_ps, count(tile))
                return tile, 1, lambda c: att_bank(tile, "attn")[:, chunk(c)]

            def x1_norm(tile):
                wait(dve, x1_done, count(tile))
                return tile, 2, lambda c: x1[tile[1]][:, c, :]

            def x2_normed(tile):
                wait(dve, ln_rstd[2], count(tile))
                wait(dve, x2T_ps, count(before(tile)))
                for c in range(CHUNKS):
                    last = nc.vector.tensor_scalar(x2[:, c, :], x1[tile[1]][:, c, :], mean_var[:, 2, c, 0:1],
                                                   rstd[:, 2, c:c + 1], sub, mult)
                last.then_inc(x2_done, 1)

            def x2T_low(tile):
                wait(dve, x2T_hi_done, count(tile))
                lo_part(x2T_lo[:], ps_att[0][:], x2T_hi[:], x2T_lo_done)

            def silu_gate(tile, m):
                wait(dve, tanh_done, count(tile, K, m + 1))
                wait(dve, silu_done, count(tile, K, m - 1))
                nc.vector.scalar_tensor_tensor(gate[m % 2][:], tanh_z[m % 2][:], 1.0, ps_z[m % 2][0][:], add, mult).then_inc(gate_done, 1)

            def silu_times(tile, m):
                wait(dve, gate_done, count(tile, K, m + 1))
                wait(dve, ha_hi_done, count(tile, K, m - 1))
                wait(dve, ha_lo_done, count(tile, K, m - 1))
                nc.vector.scalar_tensor_tensor(h_a[m % 2][:], gate[m % 2][:], silu_s[:, m:m + 1], ps_z[m % 2][1][:], mult, mult).then_inc(silu_done, 1)

            def ha_low(tile, m):
                wait(dve, ha_hi_done, count(tile, K, m + 1))
                lo_part(ha_lo[:, m, :], h_a[m % 2][:], ha_hi[:, m, :], ha_lo_done)

            def gelu_low(tile, m, layer):
                hi, lo, hi_done, lo_done = ((hb_hi, hb_lo, hb_hi_done, hb_lo_last) if layer == 1
                                            else (hc_hi, hc_lo, hc_hi_done, hc_lo_last))
                wait(dve, hi_done, count(tile, K, m + 1))
                lo_part(lo[:, m, :], h_g[m][:], hi[:, m, :], lo_done)

            def ffn_norm(tile):
                wait(dve, ffn_ps, count(tile))
                return tile, 3, lambda c: ps_z[0][0][:, chunk(c)]

            def body(tile):
                ahead2, ahead1, behind = after(after(tile)), after(tile), before(tile)
                finish = not is_number(tile, 0)
                layer_stats(attn_norm(ahead1), x_norm(ahead2))
                xs_normed(ahead2)
                norm_bias(ahead1, 1)
                if finish:
                    token_stats(ffn_norm(behind))
                xs_low(ahead2)
                if finish:
                    variances((behind, 3))
                xsT_low(ahead2)
                layer_stats(x1_norm(ahead1))
                gelu_low(tile, 3, 1)
                y_low(ahead2)
                x2_normed(ahead1)
                if finish:
                    norm_bias(behind, 3)
                state_chain(ahead2)
                x2T_low(ahead1)
                scores_masked(ahead2)
                state_low(ahead2)
                scores_low(ahead2)
                silu_gate(ahead1, 0)
                silu_gate(ahead1, 1)
                silu_times(ahead1, 0)
                silu_times(ahead1, 1)
                ha_low(ahead1, 0)
                r_low(ahead2)
                ha_low(ahead1, 1)
                silu_gate(ahead1, 2)
                silu_gate(ahead1, 3)
                silu_times(ahead1, 2)
                silu_times(ahead1, 3)
                ha_low(ahead1, 2)
                ha_low(ahead1, 3)
                gelu_low(tile, 3, 2)

            def without_attention(tile):
                ahead1, behind = after(tile), before(tile)
                layer_stats(attn_norm(ahead1))
                norm_bias(ahead1, 1)
                layer_stats(x1_norm(ahead1))
                layer_stats(ffn_norm(behind))
                gelu_low(tile, 3, 1)
                x2_normed(ahead1)
                norm_bias(behind, 3)
                x2T_low(ahead1)
                for m in (0, 2):
                    silu_gate(ahead1, m)
                    silu_times(ahead1, m)
                    silu_gate(ahead1, m + 1)
                    silu_times(ahead1, m + 1)
                    ha_low(ahead1, m)
                    ha_low(ahead1, m + 1)
                gelu_low(tile, 3, 2)

            def last_body(tile):
                layer_stats(ffn_norm(before(tile)))
                norm_bias(before(tile), 3)
                gelu_low(tile, 3, 1)
                gelu_low(tile, 3, 2)

            nc.vector.memset(neg_half[:], -0.5).then_inc(consts_done, 1)
            nc.vector.memset(ones[:], 1.0).then_inc(consts_done, 1)
            nc.vector.memset(eps_col[:], EPS).then_inc(consts_done, 1)
            nc.vector.memset(state[0][:, 0, :], 0.0).then_inc(consts_done, 1)
            t0, t1 = (0, 0), (0, 1)
            dve.wait_ge(table_in, 16)
            for c in range(CHUNKS):
                nc.vector.tensor_copy(xs[:, c, P - 1:P], table[:, C_GS:C_GS + 1]).then_inc(gs_done, 1)
            dve.wait_ge(consts_done, 4)
            layer_stats(x_norm(t0))
            dve.wait_ge(attn_in, 16)
            for w, col, bias in ((wq_aug, A_Q, A_BQ), (wk_aug, A_K, A_BK)):
                nc.vector.tensor_copy(w[:, P - 1:P], attn_w[:, bias:bias + 1]).then_inc(aug_done, 1)
                nc.vector.tensor_scalar(w[:, 0:P - 1], attn_w[:, col:col + P - 1], attn_w[:, col + P - 1:col + P],
                                        None, sub).then_inc(aug_done, 1)
            nc.vector.tensor_scalar(wv_aug[:], attn_w[:, A_V:A_V + P], attn_w[:, A_V + P - 1:A_V + P],
                                    None, sub).then_inc(aug_done, 1)
            dve.wait_ge(gs_done, CHUNKS)
            xs_normed(t0)
            dve.wait_ge(av_ps, 2)
            nc.vector.tensor_copy(a_hi[:], ps_z[1][0][:, 0:P]).then_inc(av_done, 1)
            nc.vector.tensor_copy(v_hi[:], ps_z[1][1][:, 0:P]).then_inc(av_done, 1)
            dve.wait_ge(av_done, 2)
            nc.vector.tensor_tensor(a_lo[:], ps_z[1][0][:, 0:P], a_hi[:].bitcast(F32), sub).then_inc(av_done, 1)
            nc.vector.tensor_tensor(v_lo[:], ps_z[1][1][:, 0:P], v_hi[:].bitcast(F32), sub).then_inc(av_done, 1)
            xsT_low(t0)
            xs_low(t0)
            token_stats(x_norm(t1))
            y_low(t0)
            state_chain(t0)
            variances((t1, 0))
            scores_masked(t0)
            state_low(t0)
            scores_low(t0)
            xs_normed(t1)
            dve.wait_ge(half_s1_done, 1)
            nc.vector.tensor_tensor(silu_s[:], half_s1[:], scales[:, S_2:S_2 + K], mult).then_inc(silu_s_done, 1)
            split_low(dve, nc.vector, 2, (0, 1))
            r_low(t0)
            xs_low(t1)
            xsT_low(t1)
            layer_stats(attn_norm(t0))
            y_low(t1)
            state_chain(t1)
            norm_bias(t0, 1)
            scores_masked(t1)
            state_low(t1)
            split_low(dve, nc.vector, 2, (2,))
            layer_stats(x1_norm(t0))
            scores_low(t1)
            split_low(dve, nc.vector, 2, (3,))
            x2_normed(t0)
            split_low(dve, nc.vector, 3)
            x2T_low(t0)
            dve.wait_ge(silu_s_done, 1)
            silu_gate(t0, 0)
            silu_times(t0, 0)
            silu_gate(t0, 1)
            silu_times(t0, 1)
            dve.wait_ge(lo_sums_done, len(PIECES))
            nc.vector.reduce_sum(lo_sum[:], lo_sums[:], axis=mybir.AxisListType.X).then_inc(lo_sum_done, 1)
            ha_low(t0, 0)
            ha_low(t0, 1)
            silu_gate(t0, 2)
            silu_times(t0, 2)
            r_low(t1)
            dve.wait_ge(flag_ps, 1)
            nc.vector.tensor_copy(flag[0:1, :], ps_h[1][0:1, 0:1]).then_inc(flag_done, 1)
            silu_gate(t0, 3)
            silu_times(t0, 3)
            ha_low(t0, 2)
            ha_low(t0, 3)
            steps(body, without_attention, last_body, dve.Fori)
            layer_stats(ffn_norm(LAST))
            dve.wait_ge(ln_rstd[3], count(LAST))
            dve.wait_ge(result_done, TILES - 1)
            dve.wait_ge(x1_late_done, TILES)
            dve.wait_ge(stored[1], (TILES // 2 - 1) * 16)
            for h in range(2):
                for c in (2 * h, 2 * h + 1):
                    last = nc.vector.tensor_scalar(ffn_n[:, c, :], ps_z[0][0][:, chunk(c)], mean_var[:, 3, c, 0:1],
                                                   rstd[:, 3, c:c + 1], sub, mult)
                last.then_inc(last_n_done, 1)
            for h in range(2):
                part = slice(2 * h, 2 * h + 2)
                dve.wait_ge(last_n_done, h + 1)
                nc.vector.tensor_tensor(result[1][:, part, :], ffn_n[:, part, :], x1_late[:, part, :], add).then_inc(last_result_done, 1)

        @block.tensor
        def _(pe):
            def product(out, left, right, start, stop, exact=False):
                terms = [(0, 0), (0, 1)] if exact else [(0, 0), (0, 1), (1, 0)]
                for n, (i, j) in enumerate(terms):
                    last = nc.tensor.matmul(out, left[i], right[j], start=start and n == 0,
                                            stop=stop and n == len(terms) - 1)
                return last

            def cut(pair, *index):
                return [t[index] for t in pair]

            every = slice(None)

            def transpose4(out, source):
                for c in range(CHUNKS):
                    last = nc.tensor.transpose(out[:, chunk(c)], source(c), table[:, C_IDENT:C_IDENT + P])
                return last

            def xs_transposed(tile):
                wait(pe, xs_done, count(tile))
                if not first_sequence(tile):
                    wait(pe, r_lo_done, count(before(tile)))
                transpose4(att_bank(tile, "x"), lambda c: xs[:, c, :]).then_inc(xsT_done, 1)

            def outer_products(tile):
                wait(pe, xs_lo_done, count(tile))
                if not first_sequence(tile):
                    wait(pe, attn_n_done, count(before(tile)))
                for c in range(CHUNKS - tile[1]):
                    x_c = cut((xs_hi, xs_lo), every, c, every)
                    last = product(att_bank(tile, "outer")[:, chunk(c)], x_c, x_c, True, True)
                last.then_inc(outer_ps, 1)

            def queries(tile):
                wait(pe, xsT_lo_done, count(tile))
                product(att_bank(tile, "y")[:], [a_hi[:], a_lo[:]], [xsT_hi[:], xsT_lo[:]], True, True).then_inc(y_ps, 1)

            def score_blocks(tile):
                wait(pe, y_lo_done, count(tile))
                if not first_sequence(tile):
                    wait(pe, state_done, count_chain(tile))
                for c in range(CHUNKS):
                    last = product(att_bank(tile, "scores")[:, chunk(c)], cut((xsT_hi, xsT_lo), every, chunk(c)),
                                   cut((y_hi, y_lo), every, chunk(c)), True, True)
                last.then_inc(scores_ps, 1)

            def retained(tile, chunks=range(CHUNKS)):
                wait(pe, scores_lo_done, count(tile))
                wait(pe, state_lo_done, count(tile))
                for c in chunks:
                    out = att_bank(tile, "r")[:, chunk(c)]
                    first = tile[1] == 0 and c == 0
                    last = product(out, cut((xs_hi, xs_lo), every, c, every),
                                   cut((scores_hi, scores_lo), every, chunk(c)), True, first)
                    if not first:
                        last = product(out, cut((state_hi, state_lo), every, c, every),
                                       cut((y_hi, y_lo), every, chunk(c)), False, True)
                if c == CHUNKS - 1:
                    last.then_inc(r_ps, 1)

            def values(tile):
                wait(pe, r_lo_done, count(tile))
                if first_sequence(tile):
                    wait(pe, attn_n_done, count(before(tile)))
                for c in range(CHUNKS):
                    last = product(att_bank(tile, "attn")[:, chunk(c)], cut((r_hi, r_lo), every, chunk(c)), [v_hi[:], v_lo[:]], True, True)
                last.then_inc(attn_ps, 1)

            def x2_transposed(tile, ahead_queries=True):
                wait(pe, x2_done, count(tile))
                wait(pe, *((y_lo_done, count(after(tile))) if ahead_queries else (r_lo_done, count(tile))))
                transpose4(ps_att[0], lambda c: x2[:, c, :]).then_inc(x2T_ps, 1)

            def keep_warm(bank, products):
                for _ in range(products):
                    nc.tensor.matmul(bank[:, 0:P], table[:, C_IDENT:C_IDENT + P], table[:, C_TRI:C_TRI + P], start=True, stop=True)

            def weight(column, m, k=0):
                at = column + k * hidden + m * P
                return [w_hi[:, at:at + P], w_lo[:, at:at + P]]

            def gated_layer(tile, m, exact=False):
                if m == 0:
                    wait(pe, x2T_lo_done, count(tile))
                    wait(pe, ffn_n_done, count((tile[0] - 1, tile[1])))
                wait(pe, silu_done, count(tile, K, m - 1))
                for i, column in enumerate((W_1, W_2)):
                    last = product(ps_z[m % 2][i][:], weight(column, m), [x2T_hi[:], x2T_lo[:]], True, True, exact)
                last.then_inc(z_ps, 1)

            def ffn_parts(exact):
                def hidden_layer(tile, m, layer, ks=range(K)):
                    if layer == 1:
                        parts, column, done = (ha_hi, ha_lo), W_H1, h1_ps
                        freed = (hb_hi_done, tile) if m >= 2 else (hc_hi_done, before(tile))
                    else:
                        parts, column, done = (hb_hi, hb_lo), W_H2, h2_ps
                        freed = (hc_hi_done, tile) if m >= 2 else (hb_hi_done, tile)
                    if layer == 1 and m == 0 and is_number(tile, 0):
                        wait(pe, r_lo_done, 2)
                    if ks[0] == 0:
                        wait(pe, freed[0], count(freed[1], K, (m - 2) % K + 1))
                    for k in ks:
                        if m == 0:
                            wait(pe, *((ha_lo_done, count(tile, K, k + 1)) if layer == 1 else low_done(1, tile, k)))
                        last = product(ps_h[m % 2][:], weight(column, m, k), cut(parts, every, k, every), k == 0, k == K - 1, exact)
                    if ks[-1] == K - 1:
                        last.then_inc(done, 1)

                def last_layer(tile):
                    wait(pe, silu_done, TILES * K if is_number(tile, TILES - 1) else count(after(tile), K, 3))
                    for k in range(K):
                        wait(pe, *low_done(2, tile, k))
                        at = W_3 + k * P
                        last = product(ps_z[0][1][:], [w_hi[:, at:at + P], w_lo[:, at:at + P]],
                                       cut((hc_hi, hc_lo), every, k, every), k == 0, k == K - 1, exact)
                    last.then_inc(w3_ps, 1)

                def ffn_transposed(tile):
                    wait(pe, ffnT_done, count(tile))
                    transpose4(ps_z[0][0], lambda c: ffnT[:, chunk(c)]).then_inc(ffn_ps, 1)

                def body(tile):
                    ahead2, ahead1, behind = after(after(tile)), after(tile), before(tile)
                    finish = not is_number(tile, 0)
                    hidden_layer(tile, 0, 1)
                    if finish:
                        last_layer(behind)
                    hidden_layer(tile, 1, 1)
                    hidden_layer(tile, 2, 1)
                    if finish:
                        ffn_transposed(behind)
                    xs_transposed(ahead2)
                    hidden_layer(tile, 3, 1)
                    outer_products(ahead2)
                    queries(ahead2)
                    hidden_layer(tile, 0, 2)
                    hidden_layer(tile, 1, 2)
                    x2_transposed(ahead1)
                    hidden_layer(tile, 2, 2, range(0, K // 2))
                    score_blocks(ahead2)
                    gated_layer(ahead1, 0, exact)
                    gated_layer(ahead1, 1, exact)
                    hidden_layer(tile, 2, 2, range(K // 2, K))
                    retained(ahead2)
                    gated_layer(ahead1, 2, exact)
                    gated_layer(ahead1, 3, exact)
                    values(ahead2)
                    hidden_layer(tile, 3, 2)

                def without_attention(tile):
                    ahead1, behind = after(tile), before(tile)
                    hidden_layer(tile, 0, 1)
                    last_layer(behind)
                    hidden_layer(tile, 1, 1)
                    hidden_layer(tile, 2, 1)
                    ffn_transposed(behind)
                    hidden_layer(tile, 3, 1)
                    hidden_layer(tile, 0, 2)
                    x2_transposed(ahead1, ahead_queries=False)
                    hidden_layer(tile, 1, 2)
                    gated_layer(ahead1, 0, exact)
                    gated_layer(ahead1, 1, exact)
                    hidden_layer(tile, 2, 2)
                    gated_layer(ahead1, 2, exact)
                    gated_layer(ahead1, 3, exact)
                    hidden_layer(tile, 3, 2)

                def last_body(tile):
                    hidden_layer(tile, 0, 1, range(0, K // 2))
                    keep_warm(ps_att[0], 7)
                    hidden_layer(tile, 0, 1, range(K // 2, K))
                    last_layer(before(tile))
                    hidden_layer(tile, 1, 1)
                    ffn_transposed(before(tile))
                    hidden_layer(tile, 2, 1)
                    hidden_layer(tile, 3, 1)
                    for m in range(K):
                        hidden_layer(tile, m, 2)

                steps(body, without_attention, last_body, pe.Fori)
                last_layer(LAST)
                ffn_transposed(LAST)

            pe.wait_ge(table_in, 16)
            keep_warm(ps_h[0], 6)
            pe.wait_ge(aug_done, 5)
            nc.tensor.matmul(ps_z[1][0][:, 0:P], wq_aug[:], wk_aug[:], start=True, stop=True).then_inc(av_ps, 1)
            nc.tensor.transpose(ps_z[1][1][:, 0:P], wv_aug[:], table[:, C_IDENT:C_IDENT + P]).then_inc(av_ps, 1)
            t0, t1 = (0, 0), (0, 1)
            keep_warm(ps_h[0], 2)
            xs_transposed(t0)
            keep_warm(ps_h[0], 6)
            pe.wait_ge(av_done, 4)
            queries(t0)
            outer_products(t0)
            score_blocks(t0)
            keep_warm(ps_h[0], 10)
            retained(t0)
            xs_transposed(t1)
            keep_warm(ps_h[1], 5)
            values(t0)
            queries(t1)
            outer_products(t1)
            score_blocks(t1)
            keep_warm(ps_z[0][0], 23)
            retained(t1, (0, 1))
            keep_warm(ps_z[0][0], 1)
            x2_transposed(t0, ahead_queries=False)
            retained(t1, (2,))
            gated_layer(t0, 0)
            gated_layer(t0, 1)
            retained(t1, (3,))
            gated_layer(t0, 2)
            pe.wait_ge(lo_sum_done, 1)
            nc.tensor.matmul(ps_h[1][0:1, 0:1], lo_sum[:], ones[:], start=True, stop=True).then_inc(flag_ps, 1)
            gated_layer(t0, 3)
            keep_warm(ps_att[0], 8)
            values(t1)
            pe.wait_ge(flag_done, 1)
            any_lo = pe.value_load(flag[0:1, 0:1].bitcast(I32))
            with pe.If(any_lo != 0):
                ffn_parts(exact=False)
            with pe.Else():
                ffn_parts(exact=True)


def kernel(**inputs):
    import concourse.bacc as _bacc
    from concourse.bass_utils import run_bass_kernel_spmd as _run

    a = {name.removeprefix("L0_"): np.asarray(value) for name, value in inputs.items()}
    batch, seq, d = a["attn_x"].shape
    hidden = a["ffn_w1_w"].shape[0]
    k = hidden // P

    def by_input(w):
        return w.T.reshape(-1, P, w.shape[0]).transpose(1, 0, 2).reshape(P, -1)

    def by_partition(s):
        return s.reshape(-1, P).T

    arrays = {
        "x": a["attn_x"].reshape(batch * seq, d),
        "table": decay_tables(),
        "attn_w": np.concatenate([a["attn_Wq"], a["attn_Wk"], a["attn_Wv"], a["attn_bq"][:, None], a["attn_bk"][:, None]], axis=1),
        "ffn_w": np.concatenate([by_input(a[f"ffn_{n}_w"]) for n in ("w1", "w2", "h1", "h2", "w3")], axis=1),
        "scales": np.concatenate([by_partition(a[f"ffn_{n}_s"]) for n in ("w1", "w2", "h1", "h2", "w3")], axis=1),
    }
    arrays = {f"in_{n}": np.ascontiguousarray(v) for n, v in arrays.items()}
    nc = _bacc.Bacc("TRN2", target_bir_lowering=False, num_devices=1)
    args = [nc.dram_tensor(n, v.shape, F32, kind="ExternalInput").ap() for n, v in arrays.items()]
    out = nc.dram_tensor("out_0", (batch * seq, d), F32, kind="ExternalOutput").ap()
    sandwich(nc, *args, out, hidden)
    r = _run(nc, [arrays], core_ids=[0])
    return r.results[0]["out_0"].reshape(batch, seq, d)
```
